# Optimizing a Trainium2 kernel written in Bass

```python
import numpy as np
import jax
import jax.numpy as jnp

def _softmax(x, axis=-1):
    return jax.nn.softmax(x, axis=axis)

def _gelu(x):
    return jax.nn.gelu(x, approximate=True)

def _silu(x):
    return jax.nn.silu(x)

def _sigmoid(x):
    return jax.nn.sigmoid(x)

def _layernorm(x, axis=-1, eps=1e-05):
    m = jnp.mean(x, axis=axis, keepdims=True)
    v = jnp.var(x, axis=axis, keepdims=True)
    return (x - m) / jnp.sqrt(v + eps)

def _scatter_add(tgt, idx, src, axis=0):
    return tgt.at[idx].add(src)

def _segment_sum(src, seg, n):
    return jax.ops.segment_sum(src, seg, n)
kernel_name = 'mk_adj_ffn_d1_adj_r2_a2baca'

def setup_inputs(seed: int=0):
    np.random.seed(seed)
    _w = jnp.asarray

    def _rec_inputs():
        import jax
        import jax.numpy as jnp
        _gk = jax.random.key(seed)
        x = -0.0002928 + 1 * jax.random.normal(jax.random.fold_in(_gk, 1), (3327, 256), jnp.float32)
        _a = jax.random.bernoulli(jax.random.fold_in(_gk, 2), 0.00240457, (3327, 3327))
        adj = _a.astype(jnp.int32)
        return (x, adj)
    x, adj = _rec_inputs()

    def _L0_gnn_setup():
        import jax, jax.numpy as jnp
        import numpy as np
        N, D_IN, D_OUT = (4096, 256, 256)
        key = jax.random.key(seed)
        ks = jax.random.split(key, 8)
        scale_in = 1.0 / np.sqrt(D_IN)
        scale_cat = 1.0 / np.sqrt(2 * D_OUT)
        return {'x': jax.random.normal(ks[0], (N, D_IN), dtype=jnp.float32), 'adj': jax.random.randint(ks[1], (N, N), 0, 2, dtype=jnp.int32), 'W_self': jax.random.uniform(ks[2], (D_IN, D_OUT), jnp.float32, -scale_in, scale_in), 'b_self': jax.random.uniform(ks[3], (D_OUT,), jnp.float32, -scale_in, scale_in), 'W_nb': jax.random.uniform(ks[4], (D_IN, D_OUT), jnp.float32, -scale_in, scale_in), 'b_nb': jax.random.uniform(ks[5], (D_OUT,), jnp.float32, -scale_in, scale_in), 'W_comb': jax.random.uniform(ks[6], (2 * D_OUT, D_OUT), jnp.float32, -scale_cat, scale_cat), 'b_comb': jax.random.uniform(ks[7], (D_OUT,), jnp.float32, -scale_cat, scale_cat)}
    _L0_gnn_all = _L0_gnn_setup()
    _L0_gnn_in = {k: v for k, v in _L0_gnn_all.items() if k in ('W_self', 'b_self', 'W_nb', 'b_nb', 'W_comb', 'b_comb')}
    del _L0_gnn_all

    def _L0_ffn_setup():
        import jax, jax.numpy as jnp
        import numpy as np
        N_DIM = 256
        HEADS = 8
        NUM_EXPERTS = 32768
        NUM_KEYS = 128
        DIM_KEY = 128
        TOPK = 16
        SCALE = 0.02
        key = jax.random.key(seed)
        k0, k1, k2, k3, k4 = jax.random.split(key, 5)
        x = jax.random.normal(k0, (1, 1024, N_DIM), dtype=jnp.float32)
        W_q = jax.random.normal(k1, (N_DIM, 2 * HEADS * DIM_KEY), dtype=jnp.float32) * SCALE
        keys = jax.random.normal(k2, (HEADS, NUM_KEYS, 2, DIM_KEY), dtype=jnp.float32) * SCALE
        down_embed = jax.random.normal(k3, (NUM_EXPERTS, N_DIM), dtype=jnp.float32) * SCALE
        up_embed = jax.random.normal(k4, (NUM_EXPERTS, N_DIM), dtype=jnp.float32) * SCALE
        return {'x': x, 'W_q': W_q, 'keys': keys, 'down_embed': down_embed, 'up_embed': up_embed}
    _L0_ffn_all = _L0_ffn_setup()
    _L0_ffn_in = {k: v for k, v in _L0_ffn_all.items() if k in ('W_q', 'keys', 'down_embed', 'up_embed')}
    del _L0_ffn_all
    return {'x': x, 'adj': adj, 'L0_gnn_W_self': _L0_gnn_in['W_self'], 'L0_gnn_b_self': _L0_gnn_in['b_self'], 'L0_gnn_W_nb': _L0_gnn_in['W_nb'], 'L0_gnn_b_nb': _L0_gnn_in['b_nb'], 'L0_gnn_W_comb': _L0_gnn_in['W_comb'], 'L0_gnn_b_comb': _L0_gnn_in['b_comb'], 'L0_ffn_W_q': _L0_ffn_in['W_q'], 'L0_ffn_keys': _L0_ffn_in['keys'], 'L0_ffn_down_embed': _L0_ffn_in['down_embed'], 'L0_ffn_up_embed': _L0_ffn_in['up_embed']}

def reference(x, adj, L0_gnn_W_self, L0_gnn_b_self, L0_gnn_W_nb, L0_gnn_b_nb, L0_gnn_W_comb, L0_gnn_b_comb, L0_ffn_W_q, L0_ffn_keys, L0_ffn_down_embed, L0_ffn_up_embed):
    import jax
    import jax.numpy as jnp

    def _L0_gnn_ref(x, adj, W_self, b_self, W_nb, b_nb, W_comb, b_comb):
        import jax, jax.numpy as jnp
        import numpy as np
        N, D_IN, D_OUT = (4096, 256, 256)
        mask = (adj > 0).astype(x.dtype)
        deg = jnp.sum(mask, axis=1, keepdims=True)
        agg = mask @ x / jnp.maximum(deg, 1.0)
        self_f = x @ W_self + b_self
        nb_f = agg @ W_nb + b_nb
        combined = jnp.concatenate([self_f, nb_f], axis=-1)
        out = combined @ W_comb + b_comb
        return jax.nn.relu(out)

    def _L0_ffn_ref(x, W_q, keys, down_embed, up_embed):
        import jax, jax.numpy as jnp
        import numpy as np
        N_DIM = 256
        HEADS = 8
        NUM_EXPERTS = 32768
        NUM_KEYS = 128
        DIM_KEY = 128
        TOPK = 16
        SCALE = 0.02
        b, n, d = x.shape
        q = (x @ W_q).reshape(b, n, 2, HEADS, DIM_KEY).transpose(2, 0, 1, 3, 4)
        sim = jnp.einsum('pbnhd,hkpd->pbnhk', q, keys)
        sx, ix = jax.lax.top_k(sim[0], TOPK)
        sy, iy = jax.lax.top_k(sim[1], TOPK)
        all_scores = (sx[..., :, None] + sy[..., None, :]).reshape(b, n, HEADS, TOPK * TOPK)
        scores, pk_idx = jax.lax.top_k(all_scores, TOPK)
        w_down = down_embed[pk_idx]
        w_up = up_embed[pk_idx]
        h = jnp.einsum('bnd,bnhkd->bnhk', x, w_down)
        h = jax.nn.gelu(h, approximate=False)
        h = jax.nn.softmax(scores, axis=-1) * h
        return jnp.einsum('bnhk,bnhkd->bnd', h, w_up)
    x = x + _L0_gnn_ref(_layernorm(x, axis=-1), adj, L0_gnn_W_self, L0_gnn_b_self, L0_gnn_W_nb, L0_gnn_b_nb, L0_gnn_W_comb, L0_gnn_b_comb)
    x = x + _L0_ffn_ref(_layernorm(x, axis=-1)[None], L0_ffn_W_q, L0_ffn_keys, L0_ffn_down_embed, L0_ffn_up_embed)[0]
    return x

_drawn_inputs = setup_inputs


def setup_inputs(seed=0):
    import zlib

    import numpy as np

    out = dict(_drawn_inputs(seed))
    spreads = {}
    factors = {'L0_gnn_b_self': 6.226,
     'L0_gnn_b_nb': 5.268,
     'L0_gnn_b_comb': 3.171,
     'L0_ffn_W_q': 8.0,
     'L0_ffn_keys': 8.0,
     'L0_ffn_down_embed': 8.0,
     'L0_ffn_up_embed': 8.0}
    for name, (base, spread) in spreads.items():
        noise = np.random.default_rng([zlib.crc32(name.encode()), seed]).standard_normal(out[name].shape)
        drawn = base * np.exp(spread * noise) if base else spread * noise
        out[name] = jnp.asarray(drawn.astype(out[name].dtype))
    for name, factor in factors.items():
        out[name] = (out[name] * factor).astype(out[name].dtype)
    return out
```

```python
from contextlib import ExitStack

import numpy as np

import concourse.bass as bass
from concourse import mybir
from concourse.alu_op_type import AluOpType as ALU

ACT = mybir.ActivationFunctionType
AX = mybir.AxisListType
F32, F16, BF16, I32 = mybir.dt.float32, mybir.dt.float16, mybir.dt.bfloat16, mybir.dt.int32

P = 128
D = 256
KD = D // P
HEADS, KEYS, TOPK = 8, 128, 16
EPS = 1e-5
UP = 2048.0
TAKEN = -(2.0 ** 127)

RECTS = [(0, 1, 16), (1, 1, 8), (2, 2, 5), (4, 4, 3), (8, 8, 1)]
SLOTS = [(i0 + a) * TOPK + b for i0, ni, nj in RECTS for a in range(ni) for b in range(nj)]
S = len(SLOTS)
assert all(i * TOPK + j in SLOTS for i in range(TOPK) for j in range(TOPK) if (i + 1) * (j + 1) <= TOPK)


def graph_and_experts(nc, x, adj_t, wself_t, wnb_t, wcomb, bcols, bcomb, wq_t, keys_t, down_t, up, out):
    N = x.shape[0]
    T = (N + P - 1) // P
    LAST = N - (T - 1) * P
    CA = 20
    PH = 2 * HEADS
    assert T % 2 == 0

    with ExitStack() as ctx:
        def sb(name, shape, dt=F32):
            return ctx.enter_context(nc.sbuf_tensor(name, shape, dt))

        def psum(name, shape, dt=F32):
            return ctx.enter_context(nc.psum_tensor(name, shape, dt))

        def sem(name):
            return ctx.enter_context(nc.semaphore(name))

        xs = sb("xs", [P, T, D])
        hi = sb("hi", [P, T, D + 2], F16)
        lo = sb("lo", [P, T, D], F16)
        x1 = sb("x1", [P, T, D])
        wsim = sb("wsim", [P, KD, PH * KEYS])
        wab = sb("wab", [P, 4, D])
        cvec = sb("cvec", [1, D])
        up_row = sb("up_row", [1, P])
        down_sb = sb("down_sb", [P, KD, S])
        up_sb = sb("up_sb", [S, D])
        ident = sb("ident", [P, P])
        neg_half = sb("neg_half", [P, T])
        eps = sb("eps", [P, T])
        gelu_all = sb("gelu_all", [P, T, S])
        wn_in = sb("wn_in", [P, KD, D])
        b_in = sb("b_in", [P, 4])
        bc_in = sb("bc_in", [1, D])
        x1_flat = x1[:].rearrange("p t d -> p (t d)")
        wq_in = x1_flat[:, 0:PH * D].rearrange("p (q d) -> p q d", q=PH)
        keys_in = x1_flat[:, PH * D:PH * (D + KEYS)].rearrange("p (q k) -> p q k", q=PH)
        ws_in = x1_flat[:, PH * (D + KEYS):PH * (D + KEYS) + KD * D].rearrange("p (k d) -> p k d", k=KD)
        wc_in = gelu_all[:].rearrange("p t s -> p (t s)")[:, 0:4 * D].rearrange("p (k d) -> p k d", k=4)
        st6 = sb("st6", [P, T, 6])
        mv = sb("mv", [P, T, 2])
        rs0 = sb("rs0", [P, T])
        rs1 = sb("rs1", [P, T])
        rs2 = sb("rs2", [P, T])
        raw = sb("raw", [P, 2, T, P], I32)
        inv = sb("inv", [P, CA, P], BF16)
        mask = sb("mask", [P, 2, T, P], F16)
        deg1 = sb("deg1", [P, 2])
        rdeg = sb("rdeg", [P, 2])
        aggn = sb("aggn", [P, D])
        xs_cur = sb("xs_cur", [P, 2, D])
        x_cur = sb("x_cur", [P, 2, D])
        lhs4 = sb("lhs4", [P, 4, P])
        r1 = sb("r1", [P, D])
        st6b = sb("st6b", [P, 6])
        mvb = sb("mvb", [P, 2])
        veps = sb("veps", [P, 1])
        rstd = sb("rstd", [P, 1])
        x2 = sb("x2", [P, D])
        x2t = sb("x2t", [P, KD, P])
        sim_sb = sb("sim_sb", [P, 2, PH, KEYS])
        hpair = sb("hpair", [P, 2, S])
        rest = sb("rest", [P, 4, KEYS])
        s16 = sb("s16", [P, 2, 2, HEADS, TOPK])
        cand = sb("cand", [P, 2, HEADS, S])
        m8 = sb("m8", [P, HEADS, 8])
        m8b = sb("m8b", [P, HEADS, 8])
        rem1 = sb("rem1", [P, HEADS, S])
        rem2 = sb("rem2", [P, HEADS, S])
        below = sb("below", [P, HEADS, S])
        e1 = sb("e1", [P, HEADS, S])
        sel = sb("sel", [P, HEADS, S])
        zsum = sb("zsum", [P, HEADS])
        zrec = sb("zrec", [P, HEADS])
        prob = sb("prob", [P, HEADS, S])
        half4 = sb("half4", [P, 4, S])
        half2 = sb("half2", [P, 2, S])
        coef = sb("coef", [P, S])
        w = sb("w", [P, S])
        wt = sb("wt", [S, P])
        out_sb = sb("out_sb", [P, 2, D])

        agg_ps = [psum(f"agg_ps{b}", [P, 512]) for b in range(2)]
        tp_ps = psum("tp_ps", [P, 4, P])
        ob_bank = psum("ob_bank", [P, 512])
        ob_ps = ob_bank[:, 0:D]
        sim_ps = [psum(f"sim_ps{b}", [P, 4, KEYS]) for b in range(2)]
        tp2_ps = psum("tp2_ps", [P, 512])
        up_ps = psum("up_ps", [P, 512])
        h_ps, wt_ps = tp2_ps[:, D:D + S], up_ps[0:S, D:D + P]

        x_in = [sem(f"x_in{q}") for q in range(2)]
        fold_in, small_in, expert_in = sem("fold_in"), sem("small_in"), sem("expert_in")
        filled, ident_ready, zeroed = sem("filled"), sem("ident_ready"), sem("zeroed")
        stat_steps, stats_x, rstd_x = sem("stat_steps"), sem("stats_x"), sem("rstd_x")
        scale_x, xs_ready, hi_ready, lo_ready = sem("scale_x"), sem("xs_ready"), sem("hi_ready"), sem("lo_ready")
        folded, fold_kept, cvec_ready = sem("folded"), sem("fold_kept"), sem("cvec_ready")
        raw_loaded, xs_loaded, x_loaded, stored = (
            [sem(f"{n}_{e}") for e in ("even", "odd")] for n in ("raw_loaded", "xs_loaded", "x_loaded", "stored"))
        inv_ready, mask_act, mask_pool = sem("inv_ready"), sem("mask_act"), sem("mask_pool")
        agg_done, deg_step, rdeg_ready, aggn_ready = sem("agg_done"), sem("deg_step"), sem("rdeg_ready"), sem("aggn_ready")
        tp_done, lhs_ready, ob_done, r1_ready, x1_ready = (
            sem("tp_done"), sem("lhs_ready"), sem("ob_done"), sem("r1_ready"), sem("x1_ready"))
        st_step, mv_ready, veps_step, rstd_ready, x2_ready = (
            sem("st_step"), sem("mv_ready"), sem("veps_step"), sem("rstd_ready"), sem("x2_ready"))
        tp2_done, x2t_ready, sim_done, sim_ready, h_done, h_ready, gelu_ready = (
            sem("tp2_done"), sem("x2t_ready"), sem("sim_done"), sem("sim_ready"), sem("h_done"), sem("h_ready"),
            sem("gelu_ready"))
        ranked, cand_ready, below_ready, e1_ready, sel_ready, z_step, zrec_ready = (
            sem("ranked"), sem("cand_ready"), sem("below_ready"), sem("e1_ready"), sem("sel_ready"), sem("z_step"),
            sem("zrec_ready"))
        steps = [sem("steps_even"), sem("steps_odd")]
        pool_step, w_ready, wt_done, wt_ready, up_done, out_ready = (
            sem("pool_step"), sem("w_ready"), sem("wt_done"), sem("wt_ready"), sem("up_done"), sem("out_ready"))
        apart_dve, apart_act, apart_pool, apart_pe = sem("apart_dve"), sem("apart_act"), sem("apart_pool"), sem("apart_pe")

        def wait_apart(eng, s, value, own):
            eng.wait_ge(s, value)
            eng.sem_inc(own, 1)

        def tiles_loop(eng, first, last, offsets, step):
            lo_i = 2 - min(offsets) + (-min(offsets)) % 2
            n2 = (T - 1 - max(offsets) - lo_i + 1) // 2
            for i in range(first, lo_i):
                step(i, i % 2, lambda off, i=i: 0 <= i + off < T)
            with eng.Fori(lo_i // 2, lo_i // 2 + n2) as pair:
                step(pair * 2, 0, lambda off: True)
                step(pair * 2 + 1, 1, lambda off: True)
            for i in range(lo_i + 2 * n2, last + 1):
                step(i, i % 2, lambda off, i=i: 0 <= i + off < T)

        def loads(t, b):
            return 8 * (t - b) + 16

        def at_least(eng, s, value):
            if type(value) is not int or value > 0:
                eng.wait_ge(s, value)

        block = ctx.enter_context(nc.Block())

        @block.sync
        def _(sp):
            half = T // 2
            sp.dma_start(xs[:, 0:half, :], x[0:half * P, :].rearrange("(t p) d -> p t d", p=P)).then_inc(x_in[0], 16)
            sp.dma_start(xs[:, half:T - 1, :],
                         x[half * P:(T - 1) * P, :].rearrange("(t p) d -> p t d", p=P)).then_inc(x_in[1], 16)
            sp.wait_ge(zeroed, 1)
            sp.dma_start(xs[0:LAST, T - 1, :], x[(T - 1) * P:N, :]).then_inc(x_in[1], 16)

            def load_raw(t, b):
                at_least(sp, inv_ready, t - 1)
                at_least(sp, mask_pool, t - 1)
                sp.dma_start(raw[:, b], adj_t[bass.ds(t, 1)].rearrange("o p c i -> (o p) c i")).then_inc(raw_loaded[b], 16)

            def load_cur(t, b):
                if type(t) is int and t == 0:
                    sp.wait_ge(lo_ready, 2)
                at_least(sp, tp_done, t - 1)
                at_least(sp, x1_ready, t - 1)
                sp.dma_start(xs_cur[:, b], xs[:, bass.ds(t, 1), :].rearrange("p o d -> p (o d)")).then_inc(xs_loaded[b], 16)
                rows = LAST if type(t) is int and t == T - 1 else P
                sp.dma_start(x_cur[0:rows, b], x[bass.ds(t * P, rows), :]).then_inc(x_loaded[b], 16)

            def store(t, b):
                sp.wait_ge(out_ready, t + 1)
                rows = LAST if type(t) is int and t == T - 1 else P
                sp.dma_start(out[bass.ds(t * P, rows), :], out_sb[0:rows, b]).then_inc(stored[b], 16)

            def step(i, b, live):
                if live(4):
                    load_raw(i + 4, b)
                if live(2):
                    load_cur(i + 2, b)
                if live(-3):
                    store(i - 3, 1 - b)

            tiles_loop(sp, -4, T + 2, (-3, 4), step)
            for b in range(2):
                sp.wait_ge(stored[b], 8 * T)

        @block.gpsimd
        def _(pool):
            pool.memset(ident[:], 0.0).then_inc(filled, 1)
            pool.memset(neg_half[:], -0.5).then_inc(filled, 1)
            pool.memset(eps[:], EPS).then_inc(filled, 1)
            pool.memset(up_row[:], UP).then_inc(filled, 1)
            pool.memset(hi[:, :, D:D + 2], 1.0).then_inc(filled, 1)
            pool.memset(x_cur[:], 0.0).then_inc(filled, 1)
            pool.wait_ge(filled, 6)
            pool.affine_select(out=ident[:], in_=ident[:], compare_op=ALU.not_equal, fill=1.0, base=0,
                               pattern=[[-1, P]], channel_multiplier=1).then_inc(ident_ready, 1)
            half = T // 2
            for q in range(2):
                r = slice(q * half, (q + 1) * half)
                pool.wait_ge(stats_x, (q + 1) * half)
                pool.tensor_tensor(rs0[:, r], mv[:, r, 1], eps[:, r], ALU.add).then_inc(rstd_x, 1)
                pool.wait_ge(rstd_x, 2 * q + 1)
                pool.tensor_tensor(rs1[:, r], rs0[:, r], neg_half[:, r], ALU.pow).then_inc(rstd_x, 1)
            pool.wait_ge(hi_ready, 2)
            pool.tensor_tensor(lo[:, half:T], xs[:, half:T], hi[:, half:T, 0:D], ALU.subtract).then_inc(lo_ready, 1)

            def pairs(t, b):
                wait_apart(pool, ranked, 4 * t + 4, apart_pool)
                slot = 0
                for i0, ni, nj in RECTS:
                    o = cand[:, b, :, slot:slot + ni * nj].rearrange("p h (i j) -> p h i j", j=nj)
                    sx = s16[:, b, 0, :, i0:i0 + ni].rearrange("p h (i o) -> p h i o", o=1)
                    sy = s16[:, b, 1, :, 0:nj].rearrange("p h (o j) -> p h o j", o=1)
                    last = pool.tensor_tensor(o, sx.to_broadcast([P, HEADS, ni, nj]),
                                              sy.to_broadcast([P, HEADS, ni, nj]), ALU.add)
                    slot += ni * nj
                last.then_inc(cand_ready, 1)
                wait_apart(pool, cand_ready, t + 1, apart_pool)
                at_least(pool, e1_ready, t)
                pool.tensor_tensor(below[:], cand[:, b], cand[:, b, :, 0:1].to_broadcast([P, HEADS, S]),
                                   ALU.subtract).then_inc(below_ready, 1)

            def weigh(t, b):
                wait_apart(pool, zrec_ready, t + 1, apart_pool)
                pool.tensor_tensor(prob[:], sel[:],
                                   zrec[:].rearrange("p (h o) -> p h o", o=1).to_broadcast([P, HEADS, S]),
                                   ALU.mult).then_inc(pool_step, 1)
                wait_apart(pool, pool_step, 4 * t + 1, apart_pool)
                pool.tensor_tensor(half4[:], prob[:, 0:4], prob[:, 4:8], ALU.add).then_inc(pool_step, 1)
                wait_apart(pool, pool_step, 4 * t + 2, apart_pool)
                pool.tensor_tensor(half2[:], half4[:, 0:2], half4[:, 2:4], ALU.add).then_inc(pool_step, 1)
                wait_apart(pool, pool_step, 4 * t + 3, apart_pool)
                pool.tensor_tensor(coef[:], half2[:, 0], half2[:, 1], ALU.add).then_inc(pool_step, 1)
                wait_apart(pool, pool_step, 4 * t + 4, apart_pool)
                if type(t) is not int or t > 0:
                    wait_apart(pool, wt_done, t, apart_pool)
                wait_apart(pool, gelu_ready, t + 2 - b, apart_pool)
                pool.tensor_tensor(w[:], coef[:], gelu_all[:, bass.ds(t, 1), :].rearrange("p o s -> p (o s)"),
                                   ALU.mult).then_inc(w_ready, 1)

            def residual(t, b):
                wait_apart(pool, r1_ready, t + 1, apart_pool)
                wait_apart(pool, x_loaded[b], loads(t, b), apart_pool)
                pool.tensor_tensor(x1[:, bass.ds(t, 1), :].rearrange("p o d -> p (o d)"), r1[:], x_cur[:, b],
                                   ALU.add).then_inc(x1_ready, 1)

            def rstd_of(t):
                wait_apart(pool, mv_ready, t + 1, apart_pool)
                pool.tensor_tensor(veps[:], mvb[:, 1:2], eps[:, 0:1], ALU.add).then_inc(veps_step, 1)
                wait_apart(pool, veps_step, t + 1, apart_pool)
                pool.tensor_tensor(rstd[:], veps[:], neg_half[:, 0:1], ALU.pow).then_inc(rstd_ready, 1)

            def mask_part(t, b):
                wait_apart(pool, raw_loaded[b], loads(t, b), apart_pool)
                if type(t) is not int or t > 1:
                    wait_apart(pool, agg_done, t - 1, apart_pool)
                pool.tensor_scalar(mask[:, b, CA:T], raw[:, b, CA:T], 1.0, 0.0, ALU.min,
                                   ALU.max).then_inc(mask_pool, 1)

            def step(i, b, live):
                if live(-1):
                    pairs(i - 1, 1 - b)
                if live(-2):
                    weigh(i - 2, b)
                if live(1):
                    residual(i + 1, 1 - b)
                    rstd_of(i + 1)
                if live(3):
                    mask_part(i + 3, 1 - b)

            tiles_loop(pool, -3, T + 1, (-2, 3), step)

        @block.scalar
        def _(act):
            act.dma_start(wc_in, wcomb.rearrange("(c p) d -> p c d", p=P)).then_inc(small_in, 16)
            act.dma_start(wn_in[:], wnb_t.rearrange("(c p) d -> p c d", p=P)).then_inc(small_in, 16)
            act.dma_start(ws_in, wself_t.rearrange("(c p) d -> p c d", p=P)).then_inc(small_in, 16)
            act.dma_start(b_in[:], bcols).then_inc(small_in, 16)
            act.dma_start(bc_in[:], bcomb).then_inc(small_in, 16)
            act.dma_start(wq_in, wq_t).then_inc(fold_in, 16)
            act.dma_start(keys_in, keys_t).then_inc(fold_in, 16)
            act.dma_start(down_sb[:], down_t.rearrange("(c p) s -> p c s", p=P)).then_inc(expert_in, 16)
            act.dma_start(up_sb[:], up).then_inc(expert_in, 16)

            act.wait_ge(folded, 1)
            act.copy(wab[:, 0:2], tp_ps[:].rearrange("p (a b) k -> p a (b k)", a=2)).then_inc(fold_kept, 1)
            act.wait_ge(folded, 2)
            act.copy(wab[:, 2:4], tp2_ps[:].rearrange("p (a d) -> p a d", a=2)).then_inc(fold_kept, 1)
            for n in range(8):
                act.wait_ge(folded, 4 + n)
                act.copy(wsim[:, n % 2, (n // 2) * 512:(n // 2 + 1) * 512],
                         sim_ps[n % 2][:].rearrange("p a k -> p (a k)")).then_inc(fold_kept, 1)

            half = T // 2
            for q in range(2):
                act.wait_ge(xs_ready, (q + 1) * half)
                act.copy(hi[:, q * half:(q + 1) * half, 0:D], xs[:, q * half:(q + 1) * half]).then_inc(hi_ready, 1)

            def mask_inv(t, b, r):
                if r == 0:
                    act.wait_ge(raw_loaded[b], loads(t, b))
                    at_least(act, mask_act, t)
                act.activation(inv[:], raw[:, b, 0:CA], ACT.Relu, bias=1.0, scale=-1.0).then_inc(inv_ready, 1)

            def mask_of(t, b):
                act.wait_ge(inv_ready, t + 1)
                at_least(act, agg_done, t - 1)
                act.activation(mask[:, b, 0:CA], inv[:], ACT.Relu, bias=1.0, scale=-1.0).then_inc(mask_act, 1)

            def mean(t, b):
                act.wait_ge(rdeg_ready, t + 1)
                act.activation(aggn[:], agg_ps[b][:, 0:D], ACT.Copy, scale=rdeg[:, b:b + 1]).then_inc(aggn_ready, 1)

            def keep_lhs(t):
                act.wait_ge(tp_done, t + 1)
                act.copy(lhs4[:], tp_ps[:]).then_inc(lhs_ready, 1)

            def relu(t):
                act.wait_ge(ob_done, t + 1)
                at_least(act, x1_ready, t)
                act.activation(r1[:], ob_ps, ACT.Relu, scale=1.0 / UP).then_inc(r1_ready, 1)

            def keep_x2t(t):
                act.wait_ge(tp2_done, t + 1)
                act.copy(x2t[:].rearrange("p k n -> p (k n)"), tp2_ps[:, 0:D]).then_inc(x2t_ready, 1)

            def keep_sim(t, b, g):
                act.wait_ge(sim_done, 4 * t + g + 1)
                at_least(act, ranked, 4 * t - 4)
                act.copy(sim_sb[:, b, 4 * g:4 * g + 4], sim_ps[g % 2][:]).then_inc(sim_ready, 1)

            def keep_h(t, b):
                act.wait_ge(h_done, t + 1)
                act.copy(hpair[:, b], h_ps).then_inc(h_ready, 1)

            def gelu_two(t):
                wait_apart(act, h_ready, t + 2, apart_act)
                act.activation(gelu_all[:, bass.ds(t, 2), :], hpair[:], ACT.Gelu).then_inc(gelu_ready, 2)

            def exp(t):
                act.wait_ge(below_ready, t + 1)
                at_least(act, sel_ready, t)
                act.activation(e1[:], below[:], ACT.Exp).then_inc(e1_ready, 1)

            def keep_wt(t):
                act.wait_ge(wt_done, t + 1)
                act.copy(wt[:], wt_ps).then_inc(wt_ready, 1)

            def step(i, b, live):
                if live(1):
                    mean(i + 1, 1 - b)
                if b and live(0):
                    gelu_two(i - 1)
                if live(1):
                    keep_lhs(i + 1)
                if live(-1):
                    exp(i - 1)
                if live(3):
                    mask_inv(i + 3, 1 - b, 0)
                if live(1):
                    relu(i + 1)
                if live(3):
                    mask_of(i + 3, 1 - b)
                if live(-2):
                    keep_wt(i - 2)
                if live(1):
                    keep_x2t(i + 1)
                    for g in range(4):
                        keep_sim(i + 1, 1 - b, g)
                    keep_h(i + 1, 1 - b)

            tiles_loop(act, -3, T + 1, (-2, 3), step)

        @block.vector
        def _(dve):
            half = T // 2
            dve.memset(xs[:, T - 1, :], 0.0).then_inc(zeroed, 1)
            for q in range(2):
                dve.wait_ge(x_in[q], 16 * (q + 1))
                for t in range(q * half, (q + 1) * half):
                    dve.bn_stats(st6[:, t], xs[:, t]).then_inc(stat_steps, 1)
                for t in range(q * half, (q + 1) * half):
                    dve.wait_ge(stat_steps, t + 1)
                    dve.bn_aggr(mv[:, t], st6[:, t]).then_inc(stats_x, 1)
                r = slice(q * half, (q + 1) * half)
                dve.wait_ge(rstd_x, 2 * q + 2)
                dve.tensor_scalar(rs2[:, r], rs1[:, r], UP, None, ALU.mult).then_inc(scale_x, 1)
                dve.wait_ge(scale_x, q + 1)
                for t in range(q * half, (q + 1) * half):
                    dve.tensor_scalar(xs[:, t], xs[:, t], mv[:, t, 0:1], rs2[:, t:t + 1], ALU.subtract,
                                      ALU.mult).then_inc(xs_ready, 1)
            dve.wait_ge(folded, 3)
            dve.wait_ge(small_in, 80)
            dve.tensor_tensor(cvec[:], up_ps[0:1, 0:D], bc_in[:], ALU.add).then_inc(cvec_ready, 1)
            dve.wait_ge(hi_ready, 1)
            dve.tensor_tensor(lo[:, 0:half], xs[:, 0:half], hi[:, 0:half, 0:D], ALU.subtract).then_inc(lo_ready, 1)

            def degree(t, b):
                dve.wait_ge(agg_done, t + 1)
                dve.tensor_scalar(deg1[:, b:b + 1], agg_ps[b][:, D:D + 1], 1.0, None, ALU.max).then_inc(deg_step, 1)
                dve.wait_ge(deg_step, t + 1)
                dve.reciprocal(rdeg[:, b:b + 1], deg1[:, b:b + 1]).then_inc(rdeg_ready, 1)

            count = [0, 0]

            def signal(ins, b):
                count[b] += 1
                ins.then_inc(steps[b], 1)
                return count[b]

            def rank(t, b, sb_, g):
                wait_apart(dve, sim_ready, 4 * t + g + 1, apart_dve)
                if type(t) is not int or t > 1:
                    wait_apart(dve, cand_ready, t - 1, apart_dve)
                rows = range(4 * g, 4 * g + 4)
                top = [s16[:, b, q // HEADS, q % HEADS] for q in rows]
                done = [signal(dve.max(top[k][:, 0:8], sim_sb[:, b, q]), sb_) for k, q in enumerate(rows)]
                for k, q in enumerate(rows):
                    dve.wait_ge(steps[sb_], done[k])
                    done[k] = signal(dve.match_replace(rest[:, k], top[k][:, 0:8], sim_sb[:, b, q], TAKEN), sb_)
                for k in range(4):
                    dve.wait_ge(steps[sb_], done[k])
                    last = dve.max(top[k][:, 8:16], rest[:, k])
                    if k < 3:
                        signal(last, sb_)
                last.then_inc(ranked, 1)

            def take(t, b, sb_):
                wait_apart(dve, cand_ready, t + 1, apart_dve)
                for h0 in (0, 4):
                    hs = range(h0, h0 + 4)
                    n = {h: signal(dve.max(m8[:, h], cand[:, b, h]), sb_) for h in hs}
                    for h in hs:
                        dve.wait_ge(steps[sb_], n[h])
                        n[h] = signal(dve.match_replace(rem1[:, h], m8[:, h], cand[:, b, h], TAKEN), sb_)
                    for h in hs:
                        dve.wait_ge(steps[sb_], n[h])
                        n[h] = signal(dve.max(m8b[:, h], rem1[:, h]), sb_)
                    for h in hs:
                        dve.wait_ge(steps[sb_], n[h])
                        n[h] = signal(dve.match_replace(rem2[:, h], m8b[:, h], rem1[:, h], TAKEN), sb_)
                dve.wait_ge(steps[sb_], n[HEADS - 1])

            def select(t):
                dve.wait_ge(e1_ready, t + 1)
                at_least(dve, w_ready, t)
                dve.scalar_tensor_tensor(out=sel[:], in0=rem2[:], scalar=TAKEN, in1=e1[:], op0=ALU.is_equal,
                                         op1=ALU.mult).then_inc(sel_ready, 1)

            def norm(t):
                dve.wait_ge(sel_ready, t + 1)
                dve.tensor_reduce(zsum[:], sel[:], AX.X, ALU.add).then_inc(z_step, 1)
                dve.wait_ge(z_step, t + 1)
                dve.reciprocal(zrec[:], zsum[:]).then_inc(zrec_ready, 1)

            def stats(t):
                wait_apart(dve, x1_ready, t + 1, apart_dve)
                dve.bn_stats(st6b[:], x1[:, bass.ds(t, 1), :].rearrange("p o d -> p (o d)")).then_inc(st_step, 1)
                wait_apart(dve, st_step, t + 1, apart_dve)
                dve.bn_aggr(mvb[:], st6b[:]).then_inc(mv_ready, 1)

            def normalise(t):
                dve.wait_ge(rstd_ready, t + 1)
                at_least(dve, tp2_done, t)
                dve.tensor_scalar(x2[:], x1[:, bass.ds(t, 1), :].rearrange("p o d -> p (o d)"), mvb[:, 0:1], rstd[:],
                                  ALU.subtract, ALU.mult).then_inc(x2_ready, 1)

            def finish(t, b):
                dve.wait_ge(up_done, t + 1)
                if type(t) is not int or t > 1:
                    dve.wait_ge(stored[b], loads(t, b) - 16)
                dve.tensor_tensor(out_sb[:, b], up_ps[:, 0:D], x1[:, bass.ds(t, 1), :].rearrange("p o d -> p (o d)"),
                                  ALU.add).then_inc(out_ready, 1)

            def step(i, b, live):
                if count[1 - b]:
                    dve.wait_ge(steps[1 - b], count[1 - b])
                    dve.sem_clear(steps[1 - b])
                count[1 - b] = 0
                count[b] = 0
                if live(1):
                    degree(i + 1, 1 - b)
                if live(0):
                    for g in range(3):
                        rank(i, b, b, g)
                if live(1):
                    stats(i + 1)
                if live(0):
                    rank(i, b, b, 3)
                if live(1):
                    normalise(i + 1)
                if live(-1):
                    take(i - 1, 1 - b, b)
                    select(i - 1)
                    norm(i - 1)
                if live(-2):
                    finish(i - 2, b)

            tiles_loop(dve, -1, T + 1, (-2, 1), step)

        @block.tensor
        def _(pe):
            pe.wait_ge(small_in, 80)
            for dst, src, c0 in ((tp_ps[:].rearrange("p (a b) k -> p a (b k)", a=2), wn_in, 2),
                                 (tp2_ps[:].rearrange("p (a d) -> p a d", a=2), ws_in, 0)):
                for m in range(KD):
                    for k in range(KD):
                        mm = pe.matmul(dst[:, m], src[:, k, m * P:(m + 1) * P], wc_in[:, c0 + k], start=(k == 0),
                                       stop=(k == KD - 1))
                mm.then_inc(folded, 1)
            for c in range(4):
                mm = pe.matmul(up_ps[0:1, 0:D], b_in[:, c:c + 1], wc_in[:, c], start=(c == 0), stop=(c == 3))
            mm.then_inc(folded, 1)
            pe.wait_ge(fold_in, 32)
            for n in range(8):
                if n > 1:
                    pe.wait_ge(fold_kept, n + 1)
                for a in range(4):
                    q = 4 * (n // 2) + a
                    mm = pe.matmul(sim_ps[n % 2][:, a], wq_in[:, q, (n % 2) * P:(n % 2 + 1) * P], keys_in[:, q],
                                   start=True, stop=True)
                mm.then_inc(folded, 1)
            pe.wait_ge(fold_kept, 10)
            pe.wait_ge(cvec_ready, 1)
            pe.wait_ge(ident_ready, 1)
            pe.wait_ge(expert_in, 32)

            def aggregate(t, b, c0, c1):
                if c0 == 0:
                    pe.wait_ge(mask_act, t + 1)
                    pe.wait_ge(mask_pool, t + 1)
                    at_least(pe, aggn_ready, t - 1)
                for c in range(c0, c1):
                    if c == 0 and type(t) is int and t == 0:
                        pe.wait_ge(hi_ready, 2)
                        pe.wait_ge(lo_ready, 2)
                    if c > 0:
                        pe.matmul(agg_ps[b][:, 0:D], mask[:, b, c], lo[:, c], start=False, stop=False)
                    mm = pe.matmul(agg_ps[b][:, 0:D + 1], mask[:, b, c], hi[:, c, 0:D + 1], start=(c == 0),
                                   stop=(c == T - 1))
                    if c == 0:
                        pe.matmul(agg_ps[b][:, 0:D], mask[:, b, c], lo[:, c], start=False, stop=False)
                return mm

            def turn(t, b):
                pe.wait_ge(aggn_ready, t + 1)
                pe.wait_ge(xs_loaded[b], loads(t, b))
                at_least(pe, lhs_ready, t)
                for k in range(KD):
                    pe.transpose(tp_ps[:, k], aggn[:, k * P:(k + 1) * P], ident[:])
                for k in range(KD):
                    mm = pe.transpose(tp_ps[:, KD + k], xs_cur[:, b, k * P:(k + 1) * P], ident[:])
                mm.then_inc(tp_done, 1)

            def combine(t):
                pe.wait_ge(lhs_ready, t + 1)
                at_least(pe, r1_ready, t)
                for q in range(4):
                    pe.matmul(ob_ps, lhs4[:, q], wab[:, q], start=(q == 0), stop=False)
                pe.matmul(ob_ps, up_row[:], cvec[:], start=False, stop=True).then_inc(ob_done, 1)

            def turn_x2(t):
                pe.wait_ge(x2_ready, t + 1)
                at_least(pe, h_ready, t)
                for k in range(KD):
                    mm = pe.transpose(tp2_ps[:, k * P:(k + 1) * P], x2[:, k * P:(k + 1) * P], ident[:])
                mm.then_inc(tp2_done, 1)

            def similar(t):
                pe.wait_ge(x2t_ready, t + 1)
                for g in range(4):
                    at_least(pe, sim_ready, 4 * t + g - 1)
                    for k in range(KD):
                        mm = pe.matmul(sim_ps[g % 2][:].rearrange("p a k -> p (a k)"), x2t[:, k],
                                       wsim[:, k, g * 512:(g + 1) * 512], start=(k == 0), stop=(k == KD - 1))
                    mm.then_inc(sim_done, 1)
                for k in range(KD):
                    mm = pe.matmul(h_ps, x2t[:, k], down_sb[:, k], start=(k == 0), stop=(k == KD - 1))
                mm.then_inc(h_done, 1)

            def turn_w(t):
                at_least(pe, out_ready, t)
                wait_apart(pe, w_ready, t + 1, apart_pe)
                pe.transpose(wt_ps, w[:], ident[:]).then_inc(wt_done, 1)

            def ascend(t):
                pe.wait_ge(wt_ready, t + 1)
                pe.matmul(up_ps[:, 0:D], wt[:], up_sb[:], start=True, stop=True).then_inc(up_done, 1)

            def step(i, b, live):
                if live(1):
                    turn(i + 1, 1 - b)
                if live(2):
                    aggregate(i + 2, b, 0, 9)
                if live(1):
                    combine(i + 1)
                if live(2):
                    aggregate(i + 2, b, 9, 18)
                if live(-2):
                    turn_w(i - 2)
                if live(2):
                    aggregate(i + 2, b, 18, T).then_inc(agg_done, 1)
                if live(1):
                    turn_x2(i + 1)
                if live(-2):
                    ascend(i - 2)
                if live(1):
                    similar(i + 1)

            tiles_loop(pe, -2, T + 1, (-2, 2), step)


def kernel(x, adj, L0_gnn_W_self, L0_gnn_b_self, L0_gnn_W_nb, L0_gnn_b_nb, L0_gnn_W_comb, L0_gnn_b_comb,
           L0_ffn_W_q, L0_ffn_keys, L0_ffn_down_embed, L0_ffn_up_embed):
    import numpy as _np
    import concourse.bacc as _bacc
    from concourse import mybir as _mybir
    from concourse.bass_utils import run_bass_kernel_spmd as _run

    x, adj = _np.asarray(x), _np.asarray(adj)
    n = x.shape[0]
    tiles = -(-n // P)
    square = _np.zeros((tiles * P, tiles * P), adj.dtype)
    square[:n, :n] = adj
    adj_t = square.reshape(tiles, P, tiles, P).transpose(0, 3, 2, 1)
    wq_t = _np.asarray(L0_ffn_W_q).T.reshape(2 * HEADS, P, D).transpose(1, 0, 2)
    keys_t = _np.asarray(L0_ffn_keys).transpose(3, 2, 0, 1).reshape(P, 2 * HEADS, KEYS)
    b_self, b_nb = _np.asarray(L0_gnn_b_self), _np.asarray(L0_gnn_b_nb)
    bcols = _np.concatenate([b_self, b_nb]).reshape(4, P).T
    given = {
        "x": x,
        "adj_t": adj_t,
        "wself_t": _np.asarray(L0_gnn_W_self).T,
        "wnb_t": _np.asarray(L0_gnn_W_nb).T,
        "wcomb": _np.asarray(L0_gnn_W_comb),
        "bcols": bcols,
        "bcomb": _np.asarray(L0_gnn_b_comb).reshape(1, D),
        "wq_t": wq_t,
        "keys_t": keys_t,
        "down_t": _np.asarray(L0_ffn_down_embed)[SLOTS].T,
        "up": _np.asarray(L0_ffn_up_embed)[SLOTS],
    }
    nc = _bacc.Bacc("TRN2", target_bir_lowering=False, num_devices=1)
    arrays, args = {}, []
    for name, a in given.items():
        a = _np.ascontiguousarray(a)
        arrays[f"in_{name}"] = a
        args.append(nc.dram_tensor(f"in_{name}", a.shape, _mybir.dt.from_np(a.dtype), kind="ExternalInput").ap())
    out = nc.dram_tensor("out_x", (n, D), _mybir.dt.float32, kind="ExternalOutput").ap()
    graph_and_experts(nc, *args, out)
    r = _run(nc, [arrays], core_ids=[0])
    return r.results[0]["out_x"]
```

```python
from contextlib import ExitStack

import numpy as np

import concourse.bass as bass
from concourse import mybir
from concourse.alu_op_type import AluOpType as ALU

ACT = mybir.ActivationFunctionType
AX = mybir.AxisListType
F32, F16, BF16, I32 = mybir.dt.float32, mybir.dt.float16, mybir.dt.bfloat16, mybir.dt.int32

P = 128
D = 256
KD = D // P
HEADS, KEYS, TOPK = 8, 128, 16
EPS = 1e-5
UP = 2048.0
TAKEN = -(2.0 ** 127)

RECTS = [(0, 1, 16), (1, 1, 8), (2, 2, 5), (4, 4, 3), (8, 8, 1)]
SLOTS = [(i0 + a) * TOPK + b for i0, ni, nj in RECTS for a in range(ni) for b in range(nj)]
S = len(SLOTS)
assert all(i * TOPK + j in SLOTS for i in range(TOPK) for j in range(TOPK) if (i + 1) * (j + 1) <= TOPK)


def graph_and_experts(nc, x, adj_t, wself_t, wnb_t, wcomb, bcols, bcomb, wq_t, keys_t, down_t, up, out):
    N = x.shape[0]
    T = (N + P - 1) // P
    LAST = N - (T - 1) * P
    CA = 20
    PH = 2 * HEADS
    assert T % 2 == 0
    GROUPS = [(T * g // 4, T * (g + 1) // 4) for g in range(4)]

    with ExitStack() as ctx:
        def sb(name, shape, dt=F32):
            return ctx.enter_context(nc.sbuf_tensor(name, shape, dt))

        def psum(name, shape, dt=F32):
            return ctx.enter_context(nc.psum_tensor(name, shape, dt))

        def sem(name):
            return ctx.enter_context(nc.semaphore(name))

        xs = sb("xs", [P, T, D])
        hi = sb("hi", [P, T, D + 2], F16)
        lo = sb("lo", [P, T, D], F16)
        x1 = sb("x1", [P, T, D])
        wsim = sb("wsim", [P, KD, PH * KEYS])
        wab = sb("wab", [P, 4, D])
        cpart = sb("cpart", [1, 3, D], BF16)
        cbias = sb("cbias", [3, D], BF16)
        up_rows = sb("up_rows", [3, P], BF16)
        down_sb = sb("down_sb", [P, KD, S])
        up_sb = sb("up_sb", [S, D])
        ident = sb("ident", [P, P])
        neg_half = sb("neg_half", [P, T])
        eps = sb("eps", [P, T])
        minus_one = sb("minus_one", [P, 1])
        gelu_all = sb("gelu_all", [P, T, S])
        wn_in = sb("wn_in", [P, KD, D])
        b_in = sb("b_in", [P, 4])
        bc_in = sb("bc_in", [1, D])
        x1_flat = x1[:].rearrange("p t d -> p (t d)")
        ws_in = x1_flat[:, 0:KD * D].rearrange("p (k d) -> p k d", k=KD)
        wq_in = x1_flat[:, KD * D:(KD + PH) * D].rearrange("p (q d) -> p q d", q=PH)
        keys_in = x1_flat[:, (KD + PH) * D:(KD + PH) * D + PH * KEYS].rearrange("p (q k) -> p q k", q=PH)
        wc_in = gelu_all[:].rearrange("p t s -> p (t s)")[:, 0:4 * D].rearrange("p (k d) -> p k d", k=4)
        st6 = sb("st6", [P, T, 6])
        mv = sb("mv", [P, T, 2])
        rs0 = sb("rs0", [P, T])
        rs1 = sb("rs1", [P, T])
        rs2 = sb("rs2", [P, T])
        raw = sb("raw", [P, 2, T, P], I32)
        inv = sb("inv", [P, CA, P], BF16)
        mask = sb("mask", [P, 2, T, P], F16)
        deg1 = sb("deg1", [P, 2])
        rdeg = sb("rdeg", [P, 2])
        aggn = sb("aggn", [P, D])
        xs_cur = sb("xs_cur", [P, 2, D])
        x_cur = sb("x_cur", [P, 2, D])
        lhs4 = sb("lhs4", [P, 4, P])
        r1 = sb("r1", [P, D])
        st6b = sb("st6b", [P, 6])
        mvb = sb("mvb", [P, 2])
        veps = sb("veps", [P, 1])
        rstd = sb("rstd", [P, 1])
        x2 = sb("x2", [P, D])
        x2t = sb("x2t", [P, KD, P])
        sim_sb = sb("sim_sb", [P, 2, PH, KEYS])
        cvec = sim_sb[0:1, 0, 0:6].rearrange("p (n a) k -> p n (a k)", n=3)
        hpair = sb("hpair", [P, 2, S])
        rest = sb("rest", [P, 4, KEYS])
        s16 = sb("s16", [P, 2, 2, HEADS, TOPK])
        cand = sb("cand", [P, 2, HEADS, S])
        top = sb("top", [P, HEADS, TOPK])
        drop = sb("drop", [P, HEADS, TOPK])
        e16 = sb("e16", [P, HEADS, TOPK])
        taken = sb("taken", [P, HEADS, S])
        rem1 = sb("rem1", [P, HEADS, S])
        rem2 = sb("rem2", [P, HEADS, S])
        below = sb("below", [P, HEADS, S])
        e1 = sb("e1", [P, HEADS, S])
        sel = sb("sel", [P, HEADS, S])
        zsum = sb("zsum", [P, HEADS])
        zrec = sb("zrec", [P, HEADS])
        prob = sb("prob", [P, HEADS, S])
        half4, half2 = sel[:, 0:4], sel[:, 4:6]
        coef = sb("coef", [P, S])
        w = sb("w", [P, S])
        wt = sb("wt", [S, P])
        up_keep = sb("up_keep", [P, D])
        out_sb = sb("out_sb", [P, 2, D])

        agg_ps = [psum(f"agg_ps{b}", [P, 512]) for b in range(2)]
        tp_ps = psum("tp_ps", [P, 4, P])
        ob_bank = psum("ob_bank", [P, 512])
        ob_ps = ob_bank[:, 0:D]
        sim_ps = [psum(f"sim_ps{b}", [P, 4, KEYS]) for b in range(2)]
        tp2_ps = psum("tp2_ps", [P, 512])
        up_ps = psum("up_ps", [P, 512])
        h_ps, wt_ps = tp2_ps[:, D:D + S], up_ps[0:S, D:D + P]

        x_in = [sem(f"x_in{g}") for g in range(len(GROUPS))]
        fold_in, small_in, expert_in = sem("fold_in"), sem("small_in"), sem("expert_in")
        filled, ident_ready, zeroed = sem("filled"), sem("ident_ready"), sem("zeroed")
        stat_steps, stats_x, rstd_x = sem("stat_steps"), sem("stats_x"), sem("rstd_x")
        scale_x, xs_ready, hi_ready, lo_ready = sem("scale_x"), sem("xs_ready"), sem("hi_ready"), sem("lo_ready")
        lo_last = sem("lo_last")
        folded, fold_kept, cvec_ready, bias_in = sem("folded"), sem("fold_kept"), sem("cvec_ready"), sem("bias_in")
        raw_loaded, xs_loaded, x_loaded, stored = (
            [sem(f"{n}_{e}") for e in ("even", "odd")] for n in ("raw_loaded", "xs_loaded", "x_loaded", "stored"))
        inv_ready, mask_act, mask_rest = sem("inv_ready"), sem("mask_act"), sem("mask_rest")
        agg_done, deg_step, rdeg_ready, aggn_ready = sem("agg_done"), sem("deg_step"), sem("rdeg_ready"), sem("aggn_ready")
        tp_done, lhs_ready, ob_done, r1_ready, x1_ready = (
            sem("tp_done"), sem("lhs_ready"), sem("ob_done"), sem("r1_ready"), sem("x1_ready"))
        st_step, mv_ready, veps_step, rstd_ready, x2_ready = (
            sem("st_step"), sem("mv_ready"), sem("veps_step"), sem("rstd_ready"), sem("x2_ready"))
        tp2_done, x2t_ready, sim_done, sim_ready, h_done, h_ready, gelu_ready = (
            sem("tp2_done"), sem("x2t_ready"), sem("sim_done"), sem("sim_ready"), sem("h_done"), sem("h_ready"),
            sem("gelu_ready"))
        ranked, cand_ready, below_ready, e1_ready, top_ready, drop_ready, e16_ready, taken_ready, z_step, zrec_ready = (
            sem("ranked"), sem("cand_ready"), sem("below_ready"), sem("e1_ready"), sem("top_ready"),
            sem("drop_ready"), sem("e16_ready"), sem("taken_ready"), sem("z_step"), sem("zrec_ready"))
        up_kept = sem("up_kept")
        steps = [sem("steps_even"), sem("steps_odd")]
        pool_step, w_ready, wt_done, wt_ready, up_done, out_ready = (
            sem("pool_step"), sem("w_ready"), sem("wt_done"), sem("wt_ready"), sem("up_done"), sem("out_ready"))
        apart_dve, apart_act, apart_pool, apart_pe = sem("apart_dve"), sem("apart_act"), sem("apart_pool"), sem("apart_pe")

        def wait_apart(eng, s, value, own):
            eng.wait_ge(s, value)
            eng.sem_inc(own, 1)

        def tiles_loop(eng, first, last, offsets, step):
            lo_i = 2 - min(offsets) + (-min(offsets)) % 2
            n2 = (T - 1 - max(offsets) - lo_i + 1) // 2
            for i in range(first, lo_i):
                step(i, i % 2, lambda off, i=i: 0 <= i + off < T)
            with eng.Fori(lo_i // 2, lo_i // 2 + n2) as pair:
                step(pair * 2, 0, lambda off: True)
                step(pair * 2 + 1, 1, lambda off: True)
            for i in range(lo_i + 2 * n2, last + 1):
                step(i, i % 2, lambda off, i=i: 0 <= i + off < T)

        def loads(t, b):
            return 8 * (t - b) + 16

        def at_least(eng, s, value):
            if type(value) is not int or value > 0:
                eng.wait_ge(s, value)

        block = ctx.enter_context(nc.Block())

        @block.sync
        def _(sp):
            def load_x(g):
                t0, t1 = GROUPS[g]
                if t1 < T:
                    sp.dma_start(xs[:, t0:t1, :],
                                 x[t0 * P:t1 * P, :].rearrange("(t p) d -> p t d", p=P)).then_inc(x_in[g], 16)
                    return
                sp.dma_start(xs[:, t0:T - 1, :],
                             x[t0 * P:(T - 1) * P, :].rearrange("(t p) d -> p t d", p=P)).then_inc(x_in[g], 16)
                sp.wait_ge(zeroed, 1)
                sp.dma_start(xs[0:LAST, T - 1, :], x[(T - 1) * P:N, :]).then_inc(x_in[g], 16)

            def load_small():
                sp.dma_start(wc_in, wcomb.rearrange("(c p) d -> p c d", p=P)).then_inc(small_in, 16)
                sp.dma_start(wn_in[:], wnb_t.rearrange("(c p) d -> p c d", p=P)).then_inc(small_in, 16)
                sp.dma_start(ws_in, wself_t.rearrange("(c p) d -> p c d", p=P)).then_inc(small_in, 16)
                sp.dma_start(b_in[:], bcols).then_inc(small_in, 16)
                sp.dma_start(bc_in[:], bcomb).then_inc(small_in, 16)

            def spread_bias():
                sp.wait_ge(cvec_ready, 6)
                sp.dma_start(cbias[:], cpart[:]).then_inc(bias_in, 16)

            def load_raw(t, b):
                at_least(sp, inv_ready, t - 1)
                at_least(sp, mask_rest, t - 1)
                sp.dma_start(raw[:, b], adj_t[bass.ds(t, 1)].rearrange("o p c i -> (o p) c i")).then_inc(raw_loaded[b], 16)

            def load_cur(t, b):
                if type(t) is int and t == 0:
                    sp.wait_ge(xs_ready, T)
                at_least(sp, tp_done, t - 1)
                at_least(sp, x1_ready, t - 1)
                sp.dma_start(xs_cur[:, b], xs[:, bass.ds(t, 1), :].rearrange("p o d -> p (o d)")).then_inc(xs_loaded[b], 16)
                rows = LAST if type(t) is int and t == T - 1 else P
                sp.dma_start(x_cur[0:rows, b], x[bass.ds(t * P, rows), :]).then_inc(x_loaded[b], 16)

            def store(t, b):
                sp.wait_ge(out_ready, t + 1)
                rows = LAST if type(t) is int and t == T - 1 else P
                sp.dma_start(out[bass.ds(t * P, rows), :], out_sb[0:rows, b]).then_inc(stored[b], 16)

            def step(i, b, live):
                if live(5):
                    load_raw(i + 5, 1 - b)
                if live(3) and not (type(i) is int and i == -3):
                    load_cur(i + 3, 1 - b)
                if live(-4):
                    store(i - 4, b)

            load_x(0)
            load_x(1)
            load_small()
            load_x(2)
            load_x(3)
            load_raw(0, 0)
            load_raw(1, 1)
            sp.dma_start(wq_in, wq_t).then_inc(fold_in, 16)
            sp.dma_start(keys_in, keys_t).then_inc(fold_in, 16)
            sp.dma_start(down_sb[:], down_t.rearrange("(c p) s -> p c s", p=P)).then_inc(expert_in, 16)
            sp.dma_start(up_sb[:], up).then_inc(expert_in, 16)
            spread_bias()
            load_cur(0, 0)
            tiles_loop(sp, -3, T + 3, (-4, 5), step)
            for b in range(2):
                sp.wait_ge(stored[b], 8 * T)

        @block.gpsimd
        def _(pool):
            pool.memset(ident[:], 0.0).then_inc(filled, 1)
            pool.memset(neg_half[:], -0.5).then_inc(filled, 1)
            pool.memset(eps[:], EPS).then_inc(filled, 1)
            pool.memset(up_rows[:], UP).then_inc(filled, 1)
            pool.memset(hi[:, :, D:D + 2], 1.0).then_inc(filled, 1)
            pool.memset(x_cur[:], 0.0).then_inc(filled, 1)
            pool.wait_ge(filled, 6)
            pool.affine_select(out=ident[:], in_=ident[:], compare_op=ALU.not_equal, fill=1.0, base=0,
                               pattern=[[-1, P]], channel_multiplier=1).then_inc(ident_ready, 1)

            def rstd_of_x(g):
                r = slice(*GROUPS[g])
                pool.wait_ge(stats_x, GROUPS[g][1])
                pool.tensor_tensor(rs0[:, r], mv[:, r, 1], eps[:, r], ALU.add).then_inc(rstd_x, 1)
                pool.wait_ge(rstd_x, 2 * g + 1)
                pool.tensor_tensor(rs1[:, r], rs0[:, r], neg_half[:, r], ALU.pow).then_inc(rstd_x, 1)

            def low_of_x(g):
                r = slice(*GROUPS[g])
                pool.wait_ge(hi_ready, g + 1)
                pool.tensor_tensor(lo[:, r], xs[:, r], hi[:, r, 0:D], ALU.subtract).then_inc(lo_ready, 1)

            def pairs(t, b):
                wait_apart(pool, ranked, 4 * t + 4, apart_pool)
                slot = 0
                for i0, ni, nj in RECTS:
                    o = cand[:, b, :, slot:slot + ni * nj].rearrange("p h (i j) -> p h i j", j=nj)
                    sx = s16[:, b, 0, :, i0:i0 + ni].rearrange("p h (i o) -> p h i o", o=1)
                    sy = s16[:, b, 1, :, 0:nj].rearrange("p h (o j) -> p h o j", o=1)
                    last = pool.tensor_tensor(o, sx.to_broadcast([P, HEADS, ni, nj]),
                                              sy.to_broadcast([P, HEADS, ni, nj]), ALU.add)
                    slot += ni * nj
                last.then_inc(cand_ready, 1)

            def fall(t, b):
                at_least(pool, e1_ready, t)
                wait_apart(pool, cand_ready, t + 1, apart_pool)
                pool.tensor_tensor(below[:], cand[:, b], cand[:, b, :, 0:1].to_broadcast([P, HEADS, S]),
                                   ALU.subtract).then_inc(below_ready, 1)

            def fall_top(t):
                at_least(pool, e16_ready, t)
                wait_apart(pool, top_ready, t + 1, apart_pool)
                pool.tensor_tensor(drop[:], top[:], top[:, :, 0:1].to_broadcast([P, HEADS, TOPK]),
                                   ALU.subtract).then_inc(drop_ready, 1)

            def weigh(t):
                def chain(n):
                    wait_apart(pool, pool_step, 5 * t + n, apart_pool)

                pool.wait_ge(e1_ready, t + 1)
                wait_apart(pool, taken_ready, t + 1, apart_pool)
                pool.tensor_tensor(sel[:], e1[:], taken[:], ALU.mult).then_inc(pool_step, 1)
                chain(1)
                wait_apart(pool, zrec_ready, t + 1, apart_pool)
                pool.tensor_tensor(prob[:], sel[:],
                                   zrec[:].rearrange("p (h o) -> p h o", o=1).to_broadcast([P, HEADS, S]),
                                   ALU.mult).then_inc(pool_step, 1)

            def sum_heads(t):
                def chain(n):
                    wait_apart(pool, pool_step, 5 * t + n, apart_pool)

                chain(2)
                pool.tensor_tensor(half4, prob[:, 0:4], prob[:, 4:8], ALU.add).then_inc(pool_step, 1)
                chain(3)
                pool.tensor_tensor(half2, half4[:, 0:2], half4[:, 2:4], ALU.add).then_inc(pool_step, 1)
                chain(4)
                pool.tensor_tensor(coef[:], half2[:, 0], half2[:, 1], ALU.add).then_inc(pool_step, 1)
                chain(5)

            def scale_by_gelu(t, b):
                at_least(pool, wt_done, t)
                wait_apart(pool, gelu_ready, t + 2 - b, apart_pool)
                pool.tensor_tensor(w[:], coef[:], gelu_all[:, bass.ds(t, 1), :].rearrange("p o s -> p (o s)"),
                                   ALU.mult).then_inc(w_ready, 1)

            def residual(t, b):
                wait_apart(pool, r1_ready, t + 1, apart_pool)
                wait_apart(pool, x_loaded[b], loads(t, b), apart_pool)
                pool.tensor_tensor(x1[:, bass.ds(t, 1), :].rearrange("p o d -> p (o d)"), r1[:], x_cur[:, b],
                                   ALU.add).then_inc(x1_ready, 1)

            def rstd_of(t):
                wait_apart(pool, mv_ready, t + 1, apart_pool)
                pool.tensor_tensor(veps[:], mvb[:, 1:2], eps[:, 0:1], ALU.add).then_inc(veps_step, 1)
                wait_apart(pool, veps_step, t + 1, apart_pool)
                pool.tensor_tensor(rstd[:], veps[:], neg_half[:, 0:1], ALU.pow).then_inc(rstd_ready, 1)

            def finish(t, b):
                if type(t) is not int or t > 1:
                    pool.wait_ge(stored[b], loads(t, b) - 16)
                wait_apart(pool, up_kept, t + 1, apart_pool)
                pool.tensor_tensor(out_sb[:, b], up_keep[:], x1[:, bass.ds(t, 1), :].rearrange("p o d -> p (o d)"),
                                   ALU.add).then_inc(out_ready, 1)

            def mask_part(t, b):
                wait_apart(pool, raw_loaded[b], loads(t, b), apart_pool)
                if type(t) is not int or t > 1:
                    wait_apart(pool, agg_done, t - 1, apart_pool)
                pool.tensor_scalar(mask[:, b, CA:T], raw[:, b, CA:T], 1.0, 0.0, ALU.min,
                                   ALU.max).then_inc(mask_rest, 1)

            def step(i, b, live):
                if live(-2):
                    fall_top(i - 2)
                if live(-1):
                    pairs(i - 1, 1 - b)
                if live(2):
                    residual(i + 2, b)
                if live(-2):
                    weigh(i - 2)
                if live(2):
                    rstd_of(i + 2)
                if live(-2):
                    sum_heads(i - 2)
                    scale_by_gelu(i - 2, b)
                if live(-3):
                    finish(i - 3, 1 - b)
                if live(-1):
                    fall(i - 1, 1 - b)
                if live(4):
                    mask_part(i + 4, b)

            rstd_of_x(0)
            rstd_of_x(1)
            low_of_x(0)
            rstd_of_x(2)
            low_of_x(1)
            rstd_of_x(3)
            low_of_x(2)
            tiles_loop(pool, -2, T + 2, (-3, 4), step)

        @block.scalar
        def _(act):
            def keep_wab():
                act.wait_ge(folded, 1)
                act.copy(wab[:, 0:2], tp_ps[:].rearrange("p (a b) k -> p a (b k)", a=2)).then_inc(fold_kept, 1)
                act.wait_ge(folded, 2)
                act.copy(wab[:, 2:4], tp2_ps[:].rearrange("p (a d) -> p a d", a=2)).then_inc(fold_kept, 1)

            def keep_wsim(n):
                act.wait_ge(folded, 4 + n)
                act.copy(wsim[:, n % 2, (n // 2) * 512:(n // 2 + 1) * 512],
                         sim_ps[n % 2][:].rearrange("p a k -> p (a k)")).then_inc(fold_kept, 1)

            def high_of_x(g):
                r = slice(*GROUPS[g])
                act.wait_ge(xs_ready, GROUPS[g][1])
                act.copy(hi[:, r, 0:D], xs[:, r]).then_inc(hi_ready, 1)

            def mask_inv(t, b):
                act.wait_ge(raw_loaded[b], loads(t, b))
                at_least(act, mask_act, t)
                act.activation(inv[:], raw[:, b, 0:CA], ACT.Relu, bias=1.0, scale=-1.0).then_inc(inv_ready, 1)

            def mask_of(t, b):
                act.wait_ge(inv_ready, t + 1)
                at_least(act, agg_done, t - 1)
                act.activation(mask[:, b, 0:CA], inv[:], ACT.Relu, bias=1.0, scale=-1.0).then_inc(mask_act, 1)

            def mean(t, b):
                act.wait_ge(rdeg_ready, t + 1)
                act.activation(aggn[:], agg_ps[b][:, 0:D], ACT.Copy, scale=rdeg[:, b:b + 1]).then_inc(aggn_ready, 1)

            def keep_lhs(t):
                act.wait_ge(tp_done, t + 1)
                act.copy(lhs4[:], tp_ps[:]).then_inc(lhs_ready, 1)

            def relu(t):
                act.wait_ge(ob_done, t + 1)
                at_least(act, x1_ready, t)
                act.activation(r1[:], ob_ps, ACT.Relu, scale=1.0 / UP).then_inc(r1_ready, 1)

            def keep_x2t(t):
                act.wait_ge(tp2_done, t + 1)
                act.copy(x2t[:].rearrange("p k n -> p (k n)"), tp2_ps[:, 0:D]).then_inc(x2t_ready, 1)

            def keep_sim(t, b, g):
                act.wait_ge(sim_done, 4 * t + g + 1)
                at_least(act, ranked, 4 * t - 4)
                act.copy(sim_sb[:, b, 4 * g:4 * g + 4], sim_ps[g % 2][:]).then_inc(sim_ready, 1)

            def keep_h(t, b):
                if b == 0:
                    at_least(act, gelu_ready, t)
                act.wait_ge(h_done, t + 1)
                act.copy(hpair[:, b], h_ps).then_inc(h_ready, 1)

            def gelu_two(t):
                wait_apart(act, h_ready, t + 2, apart_act)
                act.activation(gelu_all[:, bass.ds(t, 2), :], hpair[:], ACT.Gelu).then_inc(gelu_ready, 2)

            def exp(t):
                act.wait_ge(below_ready, t + 1)
                at_least(act, pool_step, 5 * t - 4)
                act.activation(e1[:], below[:], ACT.Exp).then_inc(e1_ready, 1)

            def exp_top(t):
                act.wait_ge(drop_ready, t + 1)
                at_least(act, z_step, t)
                act.activation(e16[:], drop[:], ACT.Exp).then_inc(e16_ready, 1)

            def mark(t):
                act.wait_ge(top_ready, t + 1)
                at_least(act, pool_step, 5 * t - 4)
                act.activation(taken[:], rem2[:], ACT.Relu, bias=minus_one[:], scale=2.0 / TAKEN).then_inc(taken_ready, 1)

            def keep_up(t):
                act.wait_ge(up_done, t + 1)
                at_least(act, out_ready, t)
                act.copy(up_keep[:], up_ps[:, 0:D]).then_inc(up_kept, 1)

            def keep_wt(t):
                act.wait_ge(wt_done, t + 1)
                act.copy(wt[:], wt_ps).then_inc(wt_ready, 1)

            def step(i, b, live):
                if live(2):
                    mean(i + 2, b)
                if live(-2):
                    exp_top(i - 2)
                    exp(i - 2)
                if live(1):
                    keep_sim(i + 1, 1 - b, 0)
                if live(2):
                    keep_lhs(i + 2)
                if live(-3):
                    keep_up(i - 3)
                if live(-2):
                    mark(i - 2)
                if live(1):
                    keep_sim(i + 1, 1 - b, 1)
                if b and live(0):
                    gelu_two(i - 1)
                if live(2):
                    relu(i + 2)
                if live(1):
                    keep_sim(i + 1, 1 - b, 2)
                    keep_sim(i + 1, 1 - b, 3)
                    keep_h(i + 1, 1 - b)
                masking = live(4)
                if masking:
                    mask_inv(i + 4, b)
                if live(2):
                    keep_x2t(i + 2)
                if masking:
                    mask_of(i + 4, b)
                if live(-2):
                    keep_wt(i - 2)

            high_of_x(0)
            keep_wab()
            high_of_x(1)
            mask_inv(0, 0)
            mask_of(0, 0)
            high_of_x(2)
            high_of_x(3)
            mask_inv(1, 1)
            mask_of(1, 1)
            mean(0, 0)
            keep_lhs(0)
            relu(0)
            for n in range(PH // 2):
                keep_wsim(n)
            keep_x2t(0)
            mask_inv(2, 0)
            mask_of(2, 0)
            tiles_loop(act, -1, T + 2, (-3, 4), step)

        @block.vector
        def _(dve):
            dve.memset(xs[:, T - 1, :], 0.0).then_inc(zeroed, 1)
            dve.memset(minus_one[:], -1.0).then_inc(zeroed, 1)

            def mask_part(t):
                dve.wait_ge(raw_loaded[t], 16)
                dve.tensor_scalar(mask[:, t, CA:T], raw[:, t, CA:T], 1.0, 0.0, ALU.min, ALU.max).then_inc(mask_rest, 1)

            def stats_of_x(g):
                t0, t1 = GROUPS[g]
                dve.wait_ge(x_in[g], 32 if t1 == T else 16)
                for t in range(t0, t1):
                    dve.bn_stats(st6[:, t], xs[:, t]).then_inc(stat_steps, 1)
                for t in range(t0, t1):
                    dve.wait_ge(stat_steps, t + 1)
                    dve.bn_aggr(mv[:, t], st6[:, t]).then_inc(stats_x, 1)

            def normalise_x(g):
                t0, t1 = GROUPS[g]
                dve.wait_ge(rstd_x, 2 * g + 2)
                dve.tensor_scalar(rs2[:, t0:t1], rs1[:, t0:t1], UP, None, ALU.mult).then_inc(scale_x, 1)
                dve.wait_ge(scale_x, g + 1)
                for t in range(t0, t1):
                    dve.tensor_scalar(xs[:, t], xs[:, t], mv[:, t, 0:1], rs2[:, t:t + 1], ALU.subtract,
                                      ALU.mult).then_inc(xs_ready, 1)

            stats_of_x(0)
            stats_of_x(1)
            normalise_x(0)
            stats_of_x(2)
            normalise_x(1)
            stats_of_x(3)
            normalise_x(2)
            mask_part(0)
            normalise_x(3)
            r = slice(*GROUPS[3])
            dve.wait_ge(hi_ready, 4)
            dve.tensor_tensor(lo[:, r], xs[:, r], hi[:, r, 0:D], ALU.subtract).then_inc(lo_last, 1)
            mask_part(1)
            dve.wait_ge(folded, 3)
            dve.wait_ge(small_in, 80)
            dve.tensor_tensor(cvec[:, 0], up_ps[0:1, 0:D], bc_in[:], ALU.add).then_inc(cvec_ready, 1)
            for n in range(3):
                dve.wait_ge(cvec_ready, 2 * n + 1)
                dve.tensor_copy(cpart[:, n], cvec[:, n]).then_inc(cvec_ready, 1)
                if n < 2:
                    dve.wait_ge(cvec_ready, 2 * n + 2)
                    dve.tensor_tensor(cvec[:, n + 1], cvec[:, n], cpart[:, n], ALU.subtract).then_inc(cvec_ready, 1)

            def degree(t, b):
                dve.wait_ge(agg_done, t + 1)
                dve.tensor_scalar(deg1[:, b:b + 1], agg_ps[b][:, D:D + 1], 1.0, None, ALU.max).then_inc(deg_step, 1)
                dve.wait_ge(deg_step, t + 1)
                dve.reciprocal(rdeg[:, b:b + 1], deg1[:, b:b + 1]).then_inc(rdeg_ready, 1)

            count = [0, 0]

            def signal(ins, b):
                count[b] += 1
                ins.then_inc(steps[b], 1)
                return count[b]

            def rank(t, b, sb_, g):
                wait_apart(dve, sim_ready, 4 * t + g + 1, apart_dve)
                if type(t) is not int or t > 1:
                    wait_apart(dve, cand_ready, t - 1, apart_dve)
                rows = range(4 * g, 4 * g + 4)
                best = [s16[:, b, q // HEADS, q % HEADS] for q in rows]
                done = [signal(dve.max(best[k][:, 0:8], sim_sb[:, b, q]), sb_) for k, q in enumerate(rows)]
                for k, q in enumerate(rows):
                    dve.wait_ge(steps[sb_], done[k])
                    done[k] = signal(dve.match_replace(rest[:, k], best[k][:, 0:8], sim_sb[:, b, q], TAKEN), sb_)
                for k in range(4):
                    dve.wait_ge(steps[sb_], done[k])
                    last = dve.max(best[k][:, 8:16], rest[:, k])
                    if k < 3:
                        signal(last, sb_)
                last.then_inc(ranked, 1)

            def take(t, b, sb_, h0):
                hs = range(h0, h0 + 4)
                if h0 == 0:
                    wait_apart(dve, cand_ready, t + 1, apart_dve)
                    if type(t) is not int or t > 0:
                        wait_apart(dve, drop_ready, t, apart_dve)
                        wait_apart(dve, taken_ready, t, apart_dve)
                n = {h: signal(dve.max(top[:, h, 0:8], cand[:, b, h]), sb_) for h in hs}
                for h in hs:
                    dve.wait_ge(steps[sb_], n[h])
                    n[h] = signal(dve.match_replace(rem1[:, h], top[:, h, 0:8], cand[:, b, h], TAKEN), sb_)
                for h in hs:
                    dve.wait_ge(steps[sb_], n[h])
                    n[h] = signal(dve.max(top[:, h, 8:16], rem1[:, h]), sb_)
                for h in hs:
                    dve.wait_ge(steps[sb_], n[h])
                    last = dve.match_replace(rem2[:, h], top[:, h, 8:16], rem1[:, h], TAKEN)
                    if h < HEADS - 1:
                        signal(last, sb_)
                if h0 + 4 == HEADS:
                    last.then_inc(top_ready, 1)

            def norm(t):
                dve.wait_ge(e16_ready, t + 1)
                dve.tensor_reduce(zsum[:], e16[:], AX.X, ALU.add).then_inc(z_step, 1)
                dve.wait_ge(z_step, t + 1)
                at_least(dve, pool_step, 5 * t - 3)
                dve.reciprocal(zrec[:], zsum[:]).then_inc(zrec_ready, 1)

            def stats(t):
                wait_apart(dve, x1_ready, t + 1, apart_dve)
                dve.bn_stats(st6b[:], x1[:, bass.ds(t, 1), :].rearrange("p o d -> p (o d)")).then_inc(st_step, 1)
                wait_apart(dve, st_step, t + 1, apart_dve)
                dve.bn_aggr(mvb[:], st6b[:]).then_inc(mv_ready, 1)

            def normalise(t):
                dve.wait_ge(rstd_ready, t + 1)
                at_least(dve, tp2_done, t)
                dve.tensor_scalar(x2[:], x1[:, bass.ds(t, 1), :].rearrange("p o d -> p (o d)"), mvb[:, 0:1], rstd[:],
                                  ALU.subtract, ALU.mult).then_inc(x2_ready, 1)

            def step(i, b, live):
                if count[1 - b]:
                    dve.wait_ge(steps[1 - b], count[1 - b])
                    dve.sem_clear(steps[1 - b])
                count[1 - b] = 0
                count[b] = 0
                if live(2):
                    degree(i + 2, b)
                if live(0):
                    rank(i, b, b, 0)
                if live(-2):
                    norm(i - 2)
                if live(0):
                    rank(i, b, b, 1)
                    rank(i, b, b, 2)
                if live(2):
                    stats(i + 2)
                if live(0):
                    rank(i, b, b, 3)
                if live(2):
                    normalise(i + 2)
                if live(-1):
                    take(i - 1, 1 - b, b, 0)
                    take(i - 1, 1 - b, b, 4)

            tiles_loop(dve, -2, T + 1, (-2, 2), step)

        @block.tensor
        def _(pe):
            pe.wait_ge(small_in, 80)
            for dst, src, c0 in ((tp_ps[:].rearrange("p (a b) k -> p a (b k)", a=2), wn_in, 2),
                                 (tp2_ps[:].rearrange("p (a d) -> p a d", a=2), ws_in, 0)):
                for m in range(KD):
                    for k in range(KD):
                        mm = pe.matmul(dst[:, m], src[:, k, m * P:(m + 1) * P], wc_in[:, c0 + k], start=(k == 0),
                                       stop=(k == KD - 1))
                mm.then_inc(folded, 1)
            for c in range(4):
                mm = pe.matmul(up_ps[0:1, 0:D], b_in[:, c:c + 1], wc_in[:, c], start=(c == 0), stop=(c == 3))
            mm.then_inc(folded, 1)

            def fold_sim(n):
                if n == 0:
                    pe.wait_ge(fold_in, 32)
                if n > 1:
                    pe.wait_ge(fold_kept, n + 1)
                for a in range(4):
                    q = 4 * (n // 2) + a
                    mm = pe.matmul(sim_ps[n % 2][:, a], wq_in[:, q, (n % 2) * P:(n % 2 + 1) * P], keys_in[:, q],
                                   start=True, stop=True)
                mm.then_inc(folded, 1)

            def aggregate(t, b, c0, c1):
                if c0 == 0:
                    pe.wait_ge(mask_act, t + 1)
                    pe.wait_ge(mask_rest, t + 1)
                    at_least(pe, aggn_ready, t - 1)
                for c in range(c0, c1):
                    if type(t) is int and t == 0:
                        for g in range(len(GROUPS)):
                            if c == GROUPS[g][0]:
                                pe.wait_ge(hi_ready, g + 1)
                                if g < 3:
                                    pe.wait_ge(lo_ready, g + 1)
                                else:
                                    pe.wait_ge(lo_last, 1)
                    if c > 0:
                        pe.matmul(agg_ps[b][:, 0:D], mask[:, b, c], lo[:, c], start=False, stop=False)
                    mm = pe.matmul(agg_ps[b][:, 0:D + 1], mask[:, b, c], hi[:, c, 0:D + 1], start=(c == 0),
                                   stop=(c == T - 1))
                    if c == 0:
                        pe.matmul(agg_ps[b][:, 0:D], mask[:, b, c], lo[:, c], start=False, stop=False)
                return mm

            def turn(t, b):
                pe.wait_ge(aggn_ready, t + 1)
                pe.wait_ge(xs_loaded[b], loads(t, b))
                at_least(pe, lhs_ready, t)
                for k in range(KD):
                    pe.transpose(tp_ps[:, k], aggn[:, k * P:(k + 1) * P], ident[:])
                for k in range(KD):
                    mm = pe.transpose(tp_ps[:, KD + k], xs_cur[:, b, k * P:(k + 1) * P], ident[:])
                mm.then_inc(tp_done, 1)

            def combine(t):
                pe.wait_ge(lhs_ready, t + 1)
                at_least(pe, r1_ready, t)
                pe.matmul(ob_ps, up_rows[:], cbias[:], start=True, stop=False)
                for q in range(4):
                    mm = pe.matmul(ob_ps, lhs4[:, q], wab[:, q], start=False, stop=(q == 3))
                mm.then_inc(ob_done, 1)

            def turn_x2(t):
                pe.wait_ge(x2_ready, t + 1)
                at_least(pe, h_ready, t)
                for k in range(KD):
                    mm = pe.transpose(tp2_ps[:, k * P:(k + 1) * P], x2[:, k * P:(k + 1) * P], ident[:])
                mm.then_inc(tp2_done, 1)

            def similar(t, gs):
                if 0 in gs:
                    pe.wait_ge(x2t_ready, t + 1)
                if type(t) is int and t == 0:
                    pe.wait_ge(fold_kept, 10)
                for g in gs:
                    at_least(pe, sim_ready, 4 * t + g - 1)
                    for k in range(KD):
                        mm = pe.matmul(sim_ps[g % 2][:].rearrange("p a k -> p (a k)"), x2t[:, k],
                                       wsim[:, k, g * 512:(g + 1) * 512], start=(k == 0), stop=(k == KD - 1))
                    mm.then_inc(sim_done, 1)

            def descend(t):
                for k in range(KD):
                    mm = pe.matmul(h_ps, x2t[:, k], down_sb[:, k], start=(k == 0), stop=(k == KD - 1))
                mm.then_inc(h_done, 1)

            def turn_w(t):
                at_least(pe, out_ready, t)
                wait_apart(pe, w_ready, t + 1, apart_pe)
                pe.transpose(wt_ps, w[:], ident[:]).then_inc(wt_done, 1)

            def ascend(t):
                pe.wait_ge(wt_ready, t + 1)
                pe.matmul(up_ps[:, 0:D], wt[:], up_sb[:], start=True, stop=True).then_inc(up_done, 1)

            def step(i, b, live):
                if live(1):
                    similar(i + 1, (0,))
                if live(2):
                    turn(i + 2, b)
                if live(-3):
                    ascend(i - 3)
                if live(1):
                    similar(i + 1, (1,))
                if live(2):
                    combine(i + 2)
                if live(1):
                    similar(i + 1, (2, 3))
                    descend(i + 1)
                if live(3):
                    aggregate(i + 3, 1 - b, 0, 13)
                if live(2):
                    turn_x2(i + 2)
                if live(3):
                    aggregate(i + 3, 1 - b, 13, T).then_inc(agg_done, 1)
                if live(-2):
                    turn_w(i - 2)

            pe.wait_ge(ident_ready, 1)
            aggregate(0, 0, 0, T).then_inc(agg_done, 1)
            aggregate(1, 1, 0, 9)
            pe.wait_ge(fold_kept, 2)
            turn(0, 0)
            aggregate(1, 1, 9, 18)
            pe.wait_ge(bias_in, 16)
            combine(0)
            aggregate(1, 1, 18, T).then_inc(agg_done, 1)
            for n in range(4):
                fold_sim(n)
            turn_x2(0)
            for n in range(4, 8):
                fold_sim(n)
            pe.wait_ge(expert_in, 32)
            tiles_loop(pe, -1, T + 2, (-3, 3), step)


def kernel(x, adj, L0_gnn_W_self, L0_gnn_b_self, L0_gnn_W_nb, L0_gnn_b_nb, L0_gnn_W_comb, L0_gnn_b_comb,
           L0_ffn_W_q, L0_ffn_keys, L0_ffn_down_embed, L0_ffn_up_embed):
    import numpy as _np
    import concourse.bacc as _bacc
    from concourse import mybir as _mybir
    from concourse.bass_utils import run_bass_kernel_spmd as _run

    x, adj = _np.asarray(x), _np.asarray(adj)
    n = x.shape[0]
    tiles = -(-n // P)
    square = _np.zeros((tiles * P, tiles * P), adj.dtype)
    square[:n, :n] = adj
    adj_t = square.reshape(tiles, P, tiles, P).transpose(0, 3, 2, 1)
    wq_t = _np.asarray(L0_ffn_W_q).T.reshape(2 * HEADS, P, D).transpose(1, 0, 2)
    keys_t = _np.asarray(L0_ffn_keys).transpose(3, 2, 0, 1).reshape(P, 2 * HEADS, KEYS)
    b_self, b_nb = _np.asarray(L0_gnn_b_self), _np.asarray(L0_gnn_b_nb)
    bcols = _np.concatenate([b_self, b_nb]).reshape(4, P).T
    given = {
        "x": x,
        "adj_t": adj_t,
        "wself_t": _np.asarray(L0_gnn_W_self).T,
        "wnb_t": _np.asarray(L0_gnn_W_nb).T,
        "wcomb": _np.asarray(L0_gnn_W_comb),
        "bcols": bcols,
        "bcomb": _np.asarray(L0_gnn_b_comb).reshape(1, D),
        "wq_t": wq_t,
        "keys_t": keys_t,
        "down_t": _np.asarray(L0_ffn_down_embed)[SLOTS].T,
        "up": _np.asarray(L0_ffn_up_embed)[SLOTS],
    }
    nc = _bacc.Bacc("TRN2", target_bir_lowering=False, num_devices=1)
    arrays, args = {}, []
    for name, a in given.items():
        a = _np.ascontiguousarray(a)
        arrays[f"in_{name}"] = a
        args.append(nc.dram_tensor(f"in_{name}", a.shape, _mybir.dt.from_np(a.dtype), kind="ExternalInput").ap())
    out = nc.dram_tensor("out_x", (n, D), _mybir.dt.float32, kind="ExternalOutput").ap()
    graph_and_experts(nc, *args, out)
    r = _run(nc, [arrays], core_ids=[0])
    return r.results[0]["out_x"]
```

```python
from contextlib import ExitStack

import numpy as np

import concourse.bass as bass
from concourse import mybir
from concourse.alu_op_type import AluOpType as ALU

ACT = mybir.ActivationFunctionType
AX = mybir.AxisListType
F32, F16, BF16, I32 = mybir.dt.float32, mybir.dt.float16, mybir.dt.bfloat16, mybir.dt.int32

P = 128
D = 256
KD = D // P
HEADS, KEYS, TOPK = 8, 128, 16
EPS = 1e-5
TINY = 1e-30
UP = 2048.0
TAKEN = -(2.0 ** 127)

RECTS = [(0, 1, 16), (1, 1, 8), (2, 1, 5), (3, 1, 4), (4, 1, 3), (5, 3, 2), (8, 8, 1)]
SLOTS = [(i0 + a) * TOPK + b for i0, ni, nj in RECTS for a in range(ni) for b in range(nj)]
S = len(SLOTS)
assert SLOTS == [i * TOPK + j for i in range(TOPK) for j in range(TOPK) if (i + 1) * (j + 1) <= TOPK]
TOP8 = 1 + max(n for n, s in enumerate(SLOTS) if (s // TOPK + 1) * (s % TOPK + 1) <= 8)


def graph_and_experts(nc, x, adj_t, wself_t, wnb_t, wcomb, bcols, bcomb, wq_t, keys_t, down_t, up, out):
    N = x.shape[0]
    T = (N + P - 1) // P
    LAST = N - (T - 1) * P
    CA = 20
    PH = 2 * HEADS
    assert T % 2 == 0
    GROUPS = [(T * g // 4, T * (g + 1) // 4) for g in range(4)]

    with ExitStack() as ctx:
        def sb(name, shape, dt=F32):
            return ctx.enter_context(nc.sbuf_tensor(name, shape, dt))

        def psum(name, shape, dt=F32):
            return ctx.enter_context(nc.psum_tensor(name, shape, dt))

        def sem(name):
            return ctx.enter_context(nc.semaphore(name))

        xs = sb("xs", [P, T, D])
        hi = sb("hi", [P, T, D + 2], F16)
        lo = sb("lo", [P, T, D], F16)
        x1 = sb("x1", [P, T, D])
        wsim_hi = sb("wsim_hi", [P, KD, PH * KEYS], F16)
        wsim_lo = sb("wsim_lo", [P, KD, PH * KEYS], F16)
        wsim_scale = sb("wsim_scale", [P, 3])
        wab = sb("wab", [P, 4, D])
        cpart = sb("cpart", [1, 3, D], BF16)
        cbias = sb("cbias", [3, D], BF16)
        up_rows = sb("up_rows", [3, P], BF16)
        down_sb = sb("down_sb", [P, KD, S])
        up_sb = sb("up_sb", [S, D])
        ident = sb("ident", [P, P])
        neg_half = sb("neg_half", [P, T])
        minus_one = sb("minus_one", [P, 1])
        gelu_all = sb("gelu_all", [P, T, S])
        b_in = sb("b_in", [P, 4])
        x1_flat = x1[:].rearrange("p t d -> p (t d)")
        ws_in = x1_flat[:, 0:KD * D].rearrange("p (k d) -> p k d", k=KD)
        wq_in = x1_flat[:, KD * D:(KD + PH) * D].rearrange("p (q d) -> p q d", q=PH)
        keys_in = x1_flat[:, (KD + PH) * D:(KD + PH) * D + PH * KEYS].rearrange("p (q k) -> p q k", q=PH)
        wc_in = gelu_all[:].rearrange("p t s -> p (t s)")[:, 0:4 * D].rearrange("p (k d) -> p k d", k=4)
        st6 = sb("st6", [P, T, 6])
        mv = sb("mv", [P, T, 2])
        rs0 = sb("rs0", [P, T])
        rs1 = sb("rs1", [P, T])
        shift_x = sb("shift_x", [P, T])
        raw = sb("raw", [P, 2, T, P], I32)
        inv = sb("inv", [P, CA, P], BF16)
        mask = sb("mask", [P, 2, T, P], F16)
        deg1 = sb("deg1", [P, 2])
        rdeg = sb("rdeg", [P, 2])
        aggn = sb("aggn", [P, D])
        xs_cur = sb("xs_cur", [P, 2, D])
        x_cur = sb("x_cur", [P, 2, D])
        lhs4 = sb("lhs4", [P, 4, P])
        r1 = sb("r1", [P, D])
        st6b = sb("st6b", [P, 6])
        mvb = sb("mvb", [P, 2])
        veps = sb("veps", [P, 1])
        rstd = sb("rstd", [P, 1])
        shift = sb("shift", [P, 1])
        x2 = sb("x2", [P, D])
        x2t = sb("x2t", [P, KD, P])
        x2t_hi = sb("x2t_hi", [P, KD, P], F16)
        x2t_lo = sb("x2t_lo", [P, KD, P], F16)
        sim_sb = sb("sim_sb", [P, 2, PH, KEYS])
        wsim = sim_sb[:].rearrange("p b q k -> p b (q k)")
        wn_in = wsim[:, 0, 0:KD * D].rearrange("p (k d) -> p k d", k=KD)
        hpair = sb("hpair", [P, 2, S])
        rest = sb("rest", [P, 4, KEYS])
        s16 = sb("s16", [P, 2, 2, HEADS, TOPK])
        cand = sb("cand", [P, 2, HEADS, S])
        cvec = cand[0:1].rearrange("p b h s -> p (b h s)")[:, 0:3 * D].rearrange("p (n d) -> p n d", n=3)
        top = sb("top", [P, HEADS, TOPK])
        drop = sb("drop", [P, HEADS, TOPK])
        e16 = sb("e16", [P, HEADS, TOPK])
        taken = sb("taken", [P, HEADS, S])
        rem1 = sb("rem1", [P, HEADS, S])
        rem2 = sb("rem2", [P, HEADS, S])
        below = sb("below", [P, HEADS, S])
        e1 = sb("e1", [P, HEADS, S])
        bc_in = e1[0:1].rearrange("p h s -> p (h s)")[:, 0:D]
        sel = sb("sel", [P, HEADS, S])
        zsum = sb("zsum", [P, HEADS])
        zrec = sb("zrec", [P, HEADS])
        prob = sb("prob", [P, HEADS, S])
        ones_row = prob[0:1].rearrange("p h s -> p (h s)")[:, 0:P]
        max8 = sb("max8", [P, PH // 2])
        max1 = sb("max1", [P, 1])
        max0 = sb("max0", [1, 1])
        half4, half2 = sel[:, 0:4], sel[:, 4:6]
        coef = sb("coef", [P, S])
        w = sb("w", [P, S])
        wt = sb("wt", [S, P])
        up_keep = sb("up_keep", [P, D])
        out_sb = sb("out_sb", [P, 2, D])

        agg_ps = [psum(f"agg_ps{b}", [P, 512]) for b in range(2)]
        tp_ps = psum("tp_ps", [P, 4, P])
        ob_bank = psum("ob_bank", [P, 512])
        ob_ps = ob_bank[:, 0:D]
        sim_ps = [psum(f"sim_ps{b}", [P, 4, KEYS]) for b in range(2)]
        tp2_ps = psum("tp2_ps", [P, 512])
        up_ps = psum("up_ps", [P, 512])
        h_ps, wt_ps = tp2_ps[:, D:D + S], up_ps[0:S, D:D + P]

        x_in = [sem(f"x_in{g}") for g in range(len(GROUPS))]
        fold_in, small_in, expert_in = sem("fold_in"), sem("small_in"), sem("expert_in")
        filled, ident_ready, zeroed = sem("filled"), sem("ident_ready"), sem("zeroed")
        stat_steps, stats_x, rstd_x = sem("stat_steps"), sem("stats_x"), sem("rstd_x")
        xs_ready, hi_ready, lo_ready = (
            [sem(f"{n}{g}") for g in range(len(GROUPS))] for n in ("xs_ready", "hi_ready", "lo_ready"))
        folded, fold_kept, cvec_ready, bias_in = sem("folded"), sem("fold_kept"), sem("cvec_ready"), sem("bias_in")
        max_step, max_turned, max_spread, scale_step, hi_split, lo_split = (
            sem("max_step"), sem("max_turned"), sem("max_spread"), sem("scale_step"), sem("hi_split"),
            sem("lo_split"))
        raw_loaded, xs_loaded, x_loaded, stored = (
            [sem(f"{n}_{e}") for e in ("even", "odd")] for n in ("raw_loaded", "xs_loaded", "x_loaded", "stored"))
        inv_ready, mask_act, mask_rest = sem("inv_ready"), sem("mask_act"), sem("mask_rest")
        agg_done, deg_step, rdeg_ready, aggn_ready = sem("agg_done"), sem("deg_step"), sem("rdeg_ready"), sem("aggn_ready")
        tp_done, lhs_ready, ob_done, r1_ready, x1_ready = (
            sem("tp_done"), sem("lhs_ready"), sem("ob_done"), sem("r1_ready"), sem("x1_ready"))
        st_step, mv_ready, veps_step, rstd_ready, x2_ready = (
            sem("st_step"), sem("mv_ready"), sem("veps_step"), sem("rstd_ready"), sem("x2_ready"))
        x2hi_ready, x2lo_ready = sem("x2hi_ready"), sem("x2lo_ready")
        tp2_done, x2t_ready, sim_done, sim_ready, h_done, h_ready, gelu_ready = (
            sem("tp2_done"), sem("x2t_ready"), sem("sim_done"), sem("sim_ready"), sem("h_done"), sem("h_ready"),
            sem("gelu_ready"))
        ranked, cand_ready, below_ready, e1_ready, top_ready, drop_ready, e16_ready, taken_ready, z_step, zrec_ready = (
            sem("ranked"), sem("cand_ready"), sem("below_ready"), sem("e1_ready"), sem("top_ready"),
            sem("drop_ready"), sem("e16_ready"), sem("taken_ready"), sem("z_step"), sem("zrec_ready"))
        up_kept = sem("up_kept")
        steps = [sem("steps_even"), sem("steps_odd")]
        last_steps = sem("last_steps")
        pool_step, w_ready, wt_done, wt_ready, up_done, out_ready = (
            sem("pool_step"), sem("w_ready"), sem("wt_done"), sem("wt_ready"), sem("up_done"), sem("out_ready"))
        apart_dve, apart_act, apart_pool, apart_pe = sem("apart_dve"), sem("apart_act"), sem("apart_pool"), sem("apart_pe")

        def wait_apart(eng, s, value, own):
            eng.wait_ge(s, value)
            eng.sem_inc(own, 1)

        def tiles_loop(eng, first, last, offsets, step):
            lo_i = 2 - min(offsets) + (-min(offsets)) % 2
            n2 = (T - 1 - max(offsets) - lo_i + 1) // 2
            for i in range(first, lo_i):
                step(i, i % 2, lambda off, i=i: 0 <= i + off < T)
            with eng.Fori(lo_i // 2, lo_i // 2 + n2) as pair:
                step(pair * 2, 0, lambda off: True)
                step(pair * 2 + 1, 1, lambda off: True)
            for i in range(lo_i + 2 * n2, last + 1):
                step(i, i % 2, lambda off, i=i: 0 <= i + off < T)

        def loads(t, b):
            return 8 * (t - b) + 16

        def at_least(eng, s, value):
            if type(value) is not int or value > 0:
                eng.wait_ge(s, value)

        block = ctx.enter_context(nc.Block())

        @block.sync
        def _(sp):
            def load_x(g):
                t0, t1 = GROUPS[g]
                if t1 < T:
                    sp.dma_start(xs[:, t0:t1, :],
                                 x[t0 * P:t1 * P, :].rearrange("(t p) d -> p t d", p=P)).then_inc(x_in[g], 16)
                    return
                sp.dma_start(xs[:, t0:T - 1, :],
                             x[t0 * P:(T - 1) * P, :].rearrange("(t p) d -> p t d", p=P)).then_inc(x_in[g], 16)
                sp.wait_ge(zeroed, 1)
                sp.dma_start(xs[0:LAST, T - 1, :], x[(T - 1) * P:N, :]).then_inc(x_in[g], 16)

            def load_small():
                sp.dma_start(wc_in, wcomb.rearrange("(c p) d -> p c d", p=P)).then_inc(small_in, 16)
                sp.dma_start(wn_in[:], wnb_t.rearrange("(c p) d -> p c d", p=P)).then_inc(small_in, 16)
                sp.dma_start(ws_in, wself_t.rearrange("(c p) d -> p c d", p=P)).then_inc(small_in, 16)
                sp.dma_start(b_in[:], bcols).then_inc(small_in, 16)
                sp.dma_start(bc_in[:], bcomb).then_inc(small_in, 16)

            def spread_bias():
                sp.wait_ge(cvec_ready, 6)
                sp.dma_start(cbias[:], cpart[:]).then_inc(bias_in, 16)

            def load_raw(t, b):
                at_least(sp, mask_act, t - 1)
                at_least(sp, mask_rest, t - 1)
                sp.dma_start(raw[:, b], adj_t[bass.ds(t, 1)].rearrange("o p c i -> (o p) c i")).then_inc(raw_loaded[b], 16)

            def load_cur(t, b):
                if type(t) is int and t == 0:
                    for ready in xs_ready:
                        sp.wait_ge(ready, 1)
                at_least(sp, tp_done, t - 1)
                at_least(sp, x1_ready, t - 1)
                sp.dma_start(xs_cur[:, b], xs[:, bass.ds(t, 1), :].rearrange("p o d -> p (o d)")).then_inc(xs_loaded[b], 16)
                rows = LAST if type(t) is int and t == T - 1 else P
                sp.dma_start(x_cur[0:rows, b], x[bass.ds(t * P, rows), :]).then_inc(x_loaded[b], 16)

            def store(t, b):
                sp.wait_ge(out_ready, t + 1)
                rows = LAST if type(t) is int and t == T - 1 else P
                sp.dma_start(out[bass.ds(t * P, rows), :], out_sb[0:rows, b]).then_inc(stored[b], 16)

            def step(i, b, live):
                if live(5):
                    load_raw(i + 5, 1 - b)
                if live(3) and not (type(i) is int and i == -3):
                    load_cur(i + 3, 1 - b)
                if live(-3):
                    store(i - 3, 1 - b)

            load_x(0)
            load_x(1)
            load_small()
            load_x(2)
            load_x(3)
            load_raw(0, 0)
            sp.dma_start(wq_in, wq_t).then_inc(fold_in, 16)
            sp.dma_start(keys_in, keys_t).then_inc(fold_in, 16)
            load_cur(0, 0)
            load_raw(1, 1)
            sp.dma_start(down_sb[:], down_t.rearrange("(c p) s -> p c s", p=P)).then_inc(expert_in, 16)
            sp.dma_start(up_sb[:], up).then_inc(expert_in, 16)
            spread_bias()
            tiles_loop(sp, -3, T + 2, (-3, 5), step)
            for b in range(2):
                sp.wait_ge(stored[b], 8 * T)

        @block.gpsimd
        def _(pool):
            pool.memset(ident[:], 0.0).then_inc(filled, 1)
            pool.memset(neg_half[:], -0.5).then_inc(filled, 1)
            pool.memset(up_rows[:], UP).then_inc(filled, 1)
            pool.memset(hi[:, :, D:D + 2], 1.0).then_inc(filled, 1)
            pool.memset(x_cur[:], 0.0).then_inc(filled, 1)
            pool.memset(ones_row, 1.0).then_inc(filled, 1)
            pool.wait_ge(filled, 6)
            pool.affine_select(out=ident[:], in_=ident[:], compare_op=ALU.not_equal, fill=1.0, base=0,
                               pattern=[[-1, P]], channel_multiplier=1).then_inc(ident_ready, 1)

            def rstd_of_x(g):
                r = slice(*GROUPS[g])
                pool.wait_ge(stats_x, GROUPS[g][1])
                pool.tensor_scalar(rs0[:, r], mv[:, r, 1], EPS, UP ** -2, ALU.add, ALU.mult).then_inc(rstd_x, 1)
                pool.wait_ge(rstd_x, 4 * g + 1)
                pool.tensor_tensor(rs1[:, r], rs0[:, r], neg_half[:, r], ALU.pow).then_inc(rstd_x, 1)
                pool.wait_ge(rstd_x, 4 * g + 2)
                pool.tensor_tensor(rs0[:, r], mv[:, r, 0], rs1[:, r], ALU.mult).then_inc(rstd_x, 1)
                pool.wait_ge(rstd_x, 4 * g + 3)
                pool.tensor_scalar(shift_x[:, r], rs0[:, r], -1.0, None, ALU.mult).then_inc(rstd_x, 1)

            def low_of_x(g):
                r = slice(*GROUPS[g])
                pool.wait_ge(hi_ready[g], 1)
                pool.tensor_tensor(lo[:, r], xs[:, r], hi[:, r, 0:D], ALU.subtract).then_inc(lo_ready[g], 1)

            def pairs(t, b):
                wait_apart(pool, ranked, 4 * t + 4, apart_pool)
                slot = 0
                for i0, ni, nj in RECTS:
                    o = cand[:, b, :, slot:slot + ni * nj].rearrange("p h (i j) -> p h i j", j=nj)
                    sx = s16[:, b, 0, :, i0:i0 + ni].rearrange("p h (i o) -> p h i o", o=1)
                    sy = s16[:, b, 1, :, 0:nj].rearrange("p h (o j) -> p h o j", o=1)
                    last = pool.tensor_tensor(o, sx.to_broadcast([P, HEADS, ni, nj]),
                                              sy.to_broadcast([P, HEADS, ni, nj]), ALU.add)
                    slot += ni * nj
                last.then_inc(cand_ready, 1)

            def fall(t, b):
                at_least(pool, e1_ready, t)
                wait_apart(pool, cand_ready, t + 1, apart_pool)
                pool.tensor_tensor(below[:], cand[:, b], cand[:, b, :, 0:1].to_broadcast([P, HEADS, S]),
                                   ALU.subtract).then_inc(below_ready, 1)

            def fall_top(t):
                at_least(pool, e16_ready, t)
                wait_apart(pool, top_ready, t + 1, apart_pool)
                pool.tensor_tensor(drop[:], top[:], top[:, :, 0:1].to_broadcast([P, HEADS, TOPK]),
                                   ALU.subtract).then_inc(drop_ready, 1)

            def weigh(t):
                pool.wait_ge(e1_ready, t + 1)
                wait_apart(pool, taken_ready, t + 1, apart_pool)
                pool.tensor_tensor(sel[:], e1[:], taken[:], ALU.mult).then_inc(pool_step, 1)

            def normalise_weights(t):
                wait_apart(pool, pool_step, 5 * t + 1, apart_pool)
                wait_apart(pool, zrec_ready, t + 1, apart_pool)
                pool.tensor_tensor(prob[:], sel[:],
                                   zrec[:].rearrange("p (h o) -> p h o", o=1).to_broadcast([P, HEADS, S]),
                                   ALU.mult).then_inc(pool_step, 1)

            def sum_heads(t):
                def chain(n):
                    wait_apart(pool, pool_step, 5 * t + n, apart_pool)

                chain(2)
                pool.tensor_tensor(half4, prob[:, 0:4], prob[:, 4:8], ALU.add).then_inc(pool_step, 1)
                chain(3)
                pool.tensor_tensor(half2, half4[:, 0:2], half4[:, 2:4], ALU.add).then_inc(pool_step, 1)
                chain(4)
                pool.tensor_tensor(coef[:], half2[:, 0], half2[:, 1], ALU.add).then_inc(pool_step, 1)
                chain(5)

            def scale_by_gelu(t, b):
                at_least(pool, wt_done, t)
                wait_apart(pool, gelu_ready, t + 2 - b, apart_pool)
                pool.tensor_tensor(w[:], coef[:], gelu_all[:, bass.ds(t, 1), :].rearrange("p o s -> p (o s)"),
                                   ALU.mult).then_inc(w_ready, 1)

            def residual(t, b):
                wait_apart(pool, r1_ready, t + 1, apart_pool)
                wait_apart(pool, x_loaded[b], loads(t, b), apart_pool)
                pool.tensor_tensor(x1[:, bass.ds(t, 1), :].rearrange("p o d -> p (o d)"), r1[:], x_cur[:, b],
                                   ALU.add).then_inc(x1_ready, 1)

            def rstd_of(t):
                at_least(pool, x2_ready, t)
                wait_apart(pool, mv_ready, t + 1, apart_pool)
                pool.tensor_scalar(veps[:], mvb[:, 1:2], EPS, UP ** -2, ALU.add, ALU.mult).then_inc(veps_step, 1)
                wait_apart(pool, veps_step, 2 * t + 1, apart_pool)
                pool.tensor_tensor(rstd[:], veps[:], neg_half[:, 0:1], ALU.pow).then_inc(veps_step, 1)
                wait_apart(pool, veps_step, 2 * t + 2, apart_pool)
                pool.tensor_scalar(shift[:], mvb[:, 0:1], rstd[:], -1.0, ALU.mult, ALU.mult).then_inc(rstd_ready, 1)

            def low_of_x2t(t):
                pool.wait_ge(x2hi_ready, t + 1)
                wait_apart(pool, x2t_ready, t + 1, apart_pool)
                pool.tensor_tensor(x2t_lo[:], x2t[:], x2t_hi[:], ALU.subtract).then_inc(x2lo_ready, 1)

            def finish(t, b):
                if type(t) is not int or t > 1:
                    pool.wait_ge(stored[b], loads(t, b) - 16)
                wait_apart(pool, up_kept, t + 1, apart_pool)
                pool.tensor_tensor(out_sb[:, b], up_keep[:], x1[:, bass.ds(t, 1), :].rearrange("p o d -> p (o d)"),
                                   ALU.add).then_inc(out_ready, 1)

            def mask_part(t, b):
                wait_apart(pool, raw_loaded[b], loads(t, b), apart_pool)
                if type(t) is not int or t > 1:
                    wait_apart(pool, agg_done, t - 1, apart_pool)
                pool.tensor_scalar(mask[:, b, CA:T], raw[:, b, CA:T], 1.0, 0.0, ALU.min,
                                   ALU.max).then_inc(mask_rest, 1)

            def step(i, b, live):
                if live(-1):
                    fall_top(i - 1)
                if live(4):
                    mask_part(i + 4, b)
                if live(0):
                    pairs(i, b)
                if live(2):
                    residual(i + 2, b)
                if live(-1) and live(0):
                    weigh(i - 1)
                if live(2):
                    rstd_of(i + 2)
                if live(-1) and live(0):
                    normalise_weights(i - 1)
                    sum_heads(i - 1)
                    scale_by_gelu(i - 1, 1 - b)
                if live(2):
                    low_of_x2t(i + 2)
                if live(0):
                    fall(i, b)
                if type(i) is int and i == T:
                    finish(i - 3, 1 - b)
                if live(-2) and not (type(i) is int and i == T - 1):
                    finish(i - 2, b)

            rstd_of_x(0)
            rstd_of_x(1)
            low_of_x(0)
            rstd_of_x(2)
            rstd_of_x(3)
            low_of_x(2)
            residual(0, 0)
            rstd_of(0)
            low_of_x2t(0)
            pool.wait_ge(mask_rest, 3)
            tiles_loop(pool, -1, T + 1, (-2, 4), step)

        @block.scalar
        def _(act):
            def keep_wab():
                act.wait_ge(folded, 1)
                act.copy(wab[:, 0:2], tp_ps[:].rearrange("p (a b) k -> p a (b k)", a=2)).then_inc(fold_kept, 1)
                act.wait_ge(folded, 2)
                act.copy(wab[:, 2:4], tp2_ps[:].rearrange("p (a d) -> p a d", a=2)).then_inc(fold_kept, 1)

            def keep_wsim(n):
                act.wait_ge(folded, 4 + n)
                act.copy(wsim[:, n % 2, (n // 2) * 512:(n // 2 + 1) * 512],
                         sim_ps[n % 2][:].rearrange("p a k -> p (a k)")).then_inc(fold_kept, 1)

            def high_of_wsim(g):
                if g == 0:
                    act.wait_ge(scale_step, 2)
                act.activation(wsim_hi[:, :, g * 512:(g + 1) * 512], wsim[:, :, g * 512:(g + 1) * 512], ACT.Copy,
                               scale=wsim_scale[:, 1:2]).then_inc(hi_split, 1)

            def normalise_x(g):
                t0, t1 = GROUPS[g]
                act.wait_ge(rstd_x, 4 * g + 4)
                for t in range(t0, t1):
                    last = act.activation(xs[:, t], xs[:, t], ACT.Identity, bias=shift_x[:, t:t + 1], scale=rs1[:, t:t + 1])
                last.then_inc(xs_ready[g], 1)

            def high_of_x(g):
                r = slice(*GROUPS[g])
                act.wait_ge(xs_ready[g], 1)
                act.copy(hi[:, r, 0:D], xs[:, r]).then_inc(hi_ready[g], 1)

            def mask_inv(t, b, part):
                if part == 0:
                    act.wait_ge(raw_loaded[b], loads(t, b))
                    at_least(act, mask_act, t)
                r = slice(part * CA // 2, (part + 1) * CA // 2)
                act.activation(inv[:, r], raw[:, b, r], ACT.Relu, bias=1.0, scale=-1.0).then_inc(inv_ready, 1)

            def mask_of(t, b):
                act.wait_ge(inv_ready, 2 * t - 4)
                at_least(act, agg_done, t - 1)
                act.activation(mask[:, b, 0:CA], inv[:], ACT.Relu, bias=1.0, scale=-1.0).then_inc(mask_act, 1)

            def mean(t, b):
                act.wait_ge(rdeg_ready, t + 1)
                act.activation(aggn[:], agg_ps[b][:, 0:D], ACT.Copy, scale=rdeg[:, b:b + 1]).then_inc(aggn_ready, 1)

            def keep_lhs(t):
                act.wait_ge(tp_done, t + 1)
                act.copy(lhs4[:], tp_ps[:]).then_inc(lhs_ready, 1)

            def relu(t):
                act.wait_ge(ob_done, t + 1)
                at_least(act, x1_ready, t)
                act.activation(r1[:], ob_ps, ACT.Relu, scale=1.0 / UP).then_inc(r1_ready, 1)

            def normalise(t):
                at_least(act, tp2_done, t)
                wait_apart(act, rstd_ready, t + 1, apart_act)
                act.activation(x2[:], x1[:, bass.ds(t, 1), :].rearrange("p o d -> p (o d)"), ACT.Identity,
                               bias=shift[:], scale=rstd[:]).then_inc(x2_ready, 1)

            def keep_x2t(t):
                act.wait_ge(tp2_done, t + 1)
                act.copy(x2t_hi[:].rearrange("p k n -> p (k n)"), tp2_ps[:, 0:D]).then_inc(x2hi_ready, 1)
                act.copy(x2t[:].rearrange("p k n -> p (k n)"), tp2_ps[:, 0:D]).then_inc(x2t_ready, 1)

            def keep_sim(t, b, g):
                act.wait_ge(sim_done, 4 * t + g + 1)
                at_least(act, ranked, 4 * t - 4)
                act.activation(sim_sb[:, b, 4 * g:4 * g + 4], sim_ps[g % 2][:], ACT.Copy,
                               scale=wsim_scale[:, 2:3]).then_inc(sim_ready, 1)

            def keep_h(t, b):
                if b == 0:
                    at_least(act, gelu_ready, t)
                act.wait_ge(h_done, t + 1)
                act.activation(hpair[:, b], h_ps, ACT.Copy, scale=1.0 / UP).then_inc(h_ready, 1)

            def gelu_two(t):
                wait_apart(act, h_ready, t + 2, apart_act)
                act.activation(gelu_all[:, bass.ds(t, 2), :], hpair[:], ACT.Gelu).then_inc(gelu_ready, 2)

            def exp(t):
                act.wait_ge(below_ready, t + 1)
                at_least(act, pool_step, 5 * t - 4)
                act.activation(e1[:], below[:], ACT.Exp).then_inc(e1_ready, 1)

            def exp_top(t):
                act.wait_ge(drop_ready, t + 1)
                at_least(act, z_step, t)
                act.activation(e16[:], drop[:], ACT.Exp).then_inc(e16_ready, 1)

            def mark(t):
                act.wait_ge(top_ready, t + 1)
                at_least(act, pool_step, 5 * t - 4)
                act.activation(taken[:], rem2[:], ACT.Relu, bias=minus_one[:], scale=2.0 / TAKEN).then_inc(taken_ready, 1)

            def keep_up(t):
                act.wait_ge(up_done, t + 1)
                at_least(act, out_ready, t)
                act.copy(up_keep[:], up_ps[:, 0:D]).then_inc(up_kept, 1)

            def keep_wt(t):
                act.wait_ge(wt_done, t + 1)
                act.copy(wt[:], wt_ps).then_inc(wt_ready, 1)

            def step(i, b, live):
                if live(1):
                    keep_sim(i + 1, 1 - b, 0)
                if live(2) and not (type(i) is int and i == -1):
                    mean(i + 2, b)
                if live(1):
                    keep_sim(i + 1, 1 - b, 1)
                if live(2):
                    keep_lhs(i + 2)
                if live(-1):
                    exp_top(i - 1)
                    exp(i - 1)
                if live(-2):
                    keep_wt(i - 2)
                if live(1):
                    keep_sim(i + 1, 1 - b, 2)
                if b and live(0):
                    gelu_two(i - 1)
                if live(2):
                    relu(i + 2)
                if live(-1):
                    mark(i - 1)
                if live(4):
                    mask_inv(i + 4, b, 0)
                    mask_inv(i + 4, b, 1)
                if live(1):
                    keep_sim(i + 1, 1 - b, 3)
                    keep_h(i + 1, 1 - b)
                if live(-2):
                    keep_up(i - 2)
                if live(2):
                    normalise(i + 2)
                    keep_x2t(i + 2)
                if live(4):
                    mask_of(i + 4, b)

            high_of_x(0)
            normalise_x(1)
            high_of_x(1)
            keep_wab()
            high_of_x(2)
            normalise_x(3)
            high_of_x(3)
            mean(0, 0)
            keep_wsim(0)
            keep_wsim(1)
            keep_lhs(0)
            keep_wsim(2)
            keep_wsim(3)
            relu(0)
            for n in range(4, PH // 2):
                keep_wsim(n)
            normalise(0)
            for g in range(4):
                high_of_wsim(g)
                if g == 0:
                    keep_x2t(0)
                if g == 3:
                    mean(1, 1)
            tiles_loop(act, -1, T + 1, (-2, 4), step)

        @block.vector
        def _(dve):
            dve.memset(xs[:, T - 1, :], 0.0).then_inc(zeroed, 1)
            dve.memset(minus_one[:], -1.0).then_inc(zeroed, 1)

            def mask_whole(t, b):
                dve.wait_ge(raw_loaded[b], loads(t, b))
                if t > 1:
                    dve.wait_ge(agg_done, t - 1)
                dve.tensor_scalar(mask[:, b, 0:CA], raw[:, b, 0:CA], 1.0, 0.0, ALU.min, ALU.max).then_inc(mask_act, 1)
                dve.tensor_scalar(mask[:, b, CA:T], raw[:, b, CA:T], 1.0, 0.0, ALU.min, ALU.max).then_inc(mask_rest, 1)

            def stats_of_x(g):
                t0, t1 = GROUPS[g]
                dve.wait_ge(x_in[g], 32 if t1 == T else 16)
                for t in range(t0, t1):
                    dve.bn_stats(st6[:, t], xs[:, t]).then_inc(stat_steps, 1)
                for t in range(t0, t1):
                    dve.wait_ge(stat_steps, t + 1)
                    dve.bn_aggr(mv[:, t], st6[:, t]).then_inc(stats_x, 1)

            def normalise_x(g):
                t0, t1 = GROUPS[g]
                dve.wait_ge(rstd_x, 4 * g + 2)
                for t in range(t0, t1):
                    last = dve.tensor_scalar(xs[:, t], xs[:, t], mv[:, t, 0:1], rs1[:, t:t + 1], ALU.subtract, ALU.mult)
                last.then_inc(xs_ready[g], 1)

            def low_of_x(g):
                r = slice(*GROUPS[g])
                dve.wait_ge(hi_ready[g], 1)
                dve.tensor_tensor(lo[:, r], xs[:, r], hi[:, r, 0:D], ALU.subtract).then_inc(lo_ready[g], 1)

            stats_of_x(0)
            stats_of_x(1)
            normalise_x(0)
            stats_of_x(2)
            stats_of_x(3)
            normalise_x(2)
            mask_whole(0, 0)
            low_of_x(1)
            low_of_x(3)
            dve.wait_ge(folded, 3)
            dve.wait_ge(small_in, 80)
            dve.tensor_tensor(cvec[:, 0], up_ps[0:1, 0:D], bc_in, ALU.add).then_inc(cvec_ready, 1)
            for n in range(3):
                dve.wait_ge(cvec_ready, 2 * n + 1)
                dve.tensor_copy(cpart[:, n], cvec[:, n]).then_inc(cvec_ready, 1)
                if n < 2:
                    dve.wait_ge(cvec_ready, 2 * n + 2)
                    dve.tensor_tensor(cvec[:, n + 1], cvec[:, n], cpart[:, n], ALU.subtract).then_inc(cvec_ready, 1)

            def largest(n):
                dve.wait_ge(fold_kept, 3 + n)
                dve.tensor_reduce(max8[:, n:n + 1], wsim[:, n % 2, (n // 2) * 512:(n // 2 + 1) * 512], AX.X, ALU.max,
                                  apply_absolute_value=True).then_inc(max_step, 1)

            def scale_wsim():
                dve.wait_ge(max_step, 8)
                dve.tensor_reduce(max1[:], max8[:], AX.X, ALU.max).then_inc(max_step, 1)
                dve.wait_ge(max_turned, 1)
                dve.tensor_reduce(max0[:], up_ps[0:1, 0:P], AX.X, ALU.max).then_inc(max_step, 1)
                dve.wait_ge(max_spread, 1)
                dve.tensor_scalar(wsim_scale[:, 0:1], up_ps[:, P:P + 1], TINY, 2.0 ** -15, ALU.max,
                                  ALU.mult).then_inc(scale_step, 1)
                dve.wait_ge(scale_step, 1)
                dve.reciprocal(wsim_scale[:, 1:2], wsim_scale[:, 0:1]).then_inc(scale_step, 1)
                dve.tensor_scalar(wsim_scale[:, 2:3], wsim_scale[:, 0:1], 1.0 / UP, None, ALU.mult).then_inc(scale_step, 1)

            def low_of_wsim(g):
                dve.wait_ge(scale_step, 3)
                dve.wait_ge(hi_split, g + 1)
                dve.scalar_tensor_tensor(out=wsim_lo[:, :, g * 512:(g + 1) * 512],
                                         in0=wsim[:, :, g * 512:(g + 1) * 512], scalar=wsim_scale[:, 1:2],
                                         in1=wsim_hi[:, :, g * 512:(g + 1) * 512], op0=ALU.mult,
                                         op1=ALU.subtract).then_inc(lo_split, 1)

            def count_neighbours(t, b):
                dve.wait_ge(agg_done, t + 1)
                dve.tensor_scalar(deg1[:, b:b + 1], agg_ps[b][:, D:D + 1], 1.0, None, ALU.max).then_inc(deg_step, 1)

            def one_over_count(t, b):
                dve.wait_ge(deg_step, t + 1)
                dve.reciprocal(rdeg[:, b:b + 1], deg1[:, b:b + 1]).then_inc(rdeg_ready, 1)

            count = [0, 0]

            def signal(ins, b):
                count[b] += 1
                ins.then_inc(steps[b], 1)
                return count[b]

            def rank(t, b, sb_, g, *others):
                others = list(others) + [None] * 3
                wait_apart(dve, sim_ready, 4 * t + g + 1, apart_dve)
                if type(t) is not int or t > 1:
                    wait_apart(dve, cand_ready, t - 1, apart_dve)
                rows = range(4 * g, 4 * g + 4)
                best = [s16[:, b, q // HEADS, q % HEADS] for q in rows]
                done = [signal(dve.max(best[k][:, 0:8], sim_sb[:, b, q]), sb_) for k, q in enumerate(rows)]
                if others[0]:
                    others[0]()
                for k, q in enumerate(rows):
                    dve.wait_ge(steps[sb_], done[k])
                    done[k] = signal(dve.match_replace(rest[:, k], best[k][:, 0:8], sim_sb[:, b, q], TAKEN), sb_)
                if others[1]:
                    others[1]()
                for k in range(4):
                    dve.wait_ge(steps[sb_], done[k])
                    last = dve.max(best[k][:, 8:16], rest[:, k])
                    if k < 3:
                        signal(last, sb_)
                last.then_inc(ranked, 1)
                if others[2]:
                    others[2]()

            def take(t, b, sb_, h0, *others):
                hs = range(h0, h0 + 4)
                if h0 == 0:
                    wait_apart(dve, cand_ready, t + 1, apart_dve)
                    if type(t) is not int or t > 0:
                        wait_apart(dve, drop_ready, t, apart_dve)
                        wait_apart(dve, taken_ready, t, apart_dve)
                n = {h: signal(dve.max(top[:, h, 0:8], cand[:, b, h, 0:TOP8]), sb_) for h in hs}
                if others:
                    others[0]()
                for h in hs:
                    dve.wait_ge(steps[sb_], n[h])
                    n[h] = signal(dve.match_replace(rem1[:, h], top[:, h, 0:8], cand[:, b, h], TAKEN), sb_)
                if others:
                    others[1]()
                for h in hs:
                    dve.wait_ge(steps[sb_], n[h])
                    n[h] = signal(dve.max(top[:, h, 8:16], rem1[:, h]), sb_)
                for h in hs:
                    dve.wait_ge(steps[sb_], n[h])
                    last = dve.match_replace(rem2[:, h], top[:, h, 8:16], rem1[:, h], TAKEN)
                    if h < HEADS - 1:
                        signal(last, sb_)
                if h0 + 4 == HEADS:
                    last.then_inc(top_ready, 1)

            def sum_top(t):
                dve.wait_ge(e16_ready, t + 1)
                dve.tensor_reduce(zsum[:], e16[:], AX.X, ALU.add).then_inc(z_step, 1)

            def one_over_sum(t):
                at_least(dve, pool_step, 5 * t - 3)
                dve.wait_ge(z_step, t + 1)
                dve.reciprocal(zrec[:], zsum[:]).then_inc(zrec_ready, 1)

            def weigh_last():
                t = T - 1
                n = 0

                def step_done(ins):
                    nonlocal n
                    n += 1
                    ins.then_inc(last_steps, 1)
                    dve.wait_ge(last_steps, n)

                dve.wait_ge(w_ready, t)
                dve.wait_ge(wt_done, t)
                dve.wait_ge(e1_ready, t + 1)
                dve.wait_ge(taken_ready, t + 1)
                dve.wait_ge(zrec_ready, t + 1)
                step_done(dve.tensor_tensor(sel[:], e1[:], taken[:], ALU.mult))
                step_done(dve.tensor_tensor(prob[:], sel[:],
                                            zrec[:].rearrange("p (h o) -> p h o", o=1).to_broadcast([P, HEADS, S]),
                                            ALU.mult))
                step_done(dve.tensor_tensor(half4, prob[:, 0:4], prob[:, 4:8], ALU.add))
                step_done(dve.tensor_tensor(half2, half4[:, 0:2], half4[:, 2:4], ALU.add))
                step_done(dve.tensor_tensor(coef[:], half2[:, 0], half2[:, 1], ALU.add))
                dve.wait_ge(gelu_ready, t + 1)
                dve.tensor_tensor(w[:], coef[:], gelu_all[:, t], ALU.mult).then_inc(w_ready, 1)

            def stats(t):
                wait_apart(dve, x1_ready, t + 1, apart_dve)
                dve.bn_stats(st6b[:], x1[:, bass.ds(t, 1), :].rearrange("p o d -> p (o d)")).then_inc(st_step, 1)

            def mean_and_variance(t):
                wait_apart(dve, st_step, t + 1, apart_dve)
                dve.bn_aggr(mvb[:], st6b[:]).then_inc(mv_ready, 1)

            def step(i, b, live):
                count[b] = 0

                def clear_other():
                    if count[1 - b]:
                        dve.wait_ge(steps[1 - b], count[1 - b])
                        dve.sem_clear(steps[1 - b])
                        count[1 - b] = 0

                if not live(1):
                    clear_other()
                if live(1):
                    rank(i + 1, 1 - b, b, 0, clear_other)
                    if live(-1):
                        rank(i + 1, 1 - b, b, 1, None, lambda: sum_top(i - 1), lambda: one_over_sum(i - 1))
                    else:
                        rank(i + 1, 1 - b, b, 1)
                elif live(-1):
                    sum_top(i - 1)
                    one_over_sum(i - 1)
                    if not live(0):
                        weigh_last()
                if live(2) and live(0):
                    take(i, b, b, 0, lambda: stats(i + 2), lambda: mean_and_variance(i + 2))
                elif live(0):
                    take(i, b, b, 0)
                elif live(2):
                    stats(i + 2)
                    mean_and_variance(i + 2)
                if live(1):
                    rank(i + 1, 1 - b, b, 2)
                if live(0):
                    take(i, b, b, 4)
                if live(3):
                    rank(i + 1, 1 - b, b, 3, lambda: count_neighbours(i + 3, 1 - b), lambda: one_over_count(i + 3, 1 - b))
                elif live(1):
                    rank(i + 1, 1 - b, b, 3)

            count_neighbours(0, 0)
            one_over_count(0, 0)
            for n in range(4):
                largest(n)
            mask_whole(1, 1)
            largest(4)
            stats(0)
            mean_and_variance(0)
            for n in range(5, PH // 2):
                largest(n)
            scale_wsim()
            mask_whole(2, 0)
            for g in range(4):
                low_of_wsim(g)
                if g == 1:
                    count_neighbours(1, 1)
                    one_over_count(1, 1)
            tiles_loop(dve, -1, T, (-1, 3), step)

        @block.tensor
        def _(pe):
            pe.wait_ge(small_in, 80)
            for dst, src, c0 in ((tp_ps[:].rearrange("p (a b) k -> p a (b k)", a=2), wn_in, 2),
                                 (tp2_ps[:].rearrange("p (a d) -> p a d", a=2), ws_in, 0)):
                for m in range(KD):
                    for k in range(KD):
                        mm = pe.matmul(dst[:, m], src[:, k, m * P:(m + 1) * P], wc_in[:, c0 + k], start=(k == 0),
                                       stop=(k == KD - 1))
                mm.then_inc(folded, 1)
            for c in range(4):
                mm = pe.matmul(up_ps[0:1, 0:D], b_in[:, c:c + 1], wc_in[:, c], start=(c == 0), stop=(c == 3))
            mm.then_inc(folded, 1)

            def fold_sim(n):
                if n == 0:
                    pe.wait_ge(fold_in, 32)
                if n > 1:
                    pe.wait_ge(fold_kept, n + 1)
                for a in range(4):
                    q = 4 * (n // 2) + a
                    mm = pe.matmul(sim_ps[n % 2][:, a], wq_in[:, q, (n % 2) * P:(n % 2 + 1) * P], keys_in[:, q],
                                   start=True, stop=True)
                mm.then_inc(folded, 1)

            def aggregate(t, b, c0, c1):
                if c0 == 0:
                    pe.wait_ge(mask_act, t + 1)
                    pe.wait_ge(mask_rest, t + 1)
                    at_least(pe, aggn_ready, t - 1)
                for c in range(c0, c1):
                    if type(t) is int and t == 0:
                        for g in range(len(GROUPS)):
                            if c == GROUPS[g][0]:
                                pe.wait_ge(hi_ready[g], 1)
                                pe.wait_ge(lo_ready[g], 1)
                    if c > 0:
                        pe.matmul(agg_ps[b][:, 0:D], mask[:, b, c], lo[:, c], start=False, stop=False)
                    mm = pe.matmul(agg_ps[b][:, 0:D + 1], mask[:, b, c], hi[:, c, 0:D + 1], start=(c == 0),
                                   stop=(c == T - 1))
                    if c == 0:
                        pe.matmul(agg_ps[b][:, 0:D], mask[:, b, c], lo[:, c], start=False, stop=False)
                return mm

            def turn(t, b):
                pe.wait_ge(aggn_ready, t + 1)
                pe.wait_ge(xs_loaded[b], loads(t, b))
                at_least(pe, lhs_ready, t)
                for k in range(KD):
                    pe.transpose(tp_ps[:, k], aggn[:, k * P:(k + 1) * P], ident[:])
                for k in range(KD):
                    mm = pe.transpose(tp_ps[:, KD + k], xs_cur[:, b, k * P:(k + 1) * P], ident[:])
                mm.then_inc(tp_done, 1)

            def combine(t):
                pe.wait_ge(lhs_ready, t + 1)
                at_least(pe, r1_ready, t)
                pe.matmul(ob_ps, up_rows[:], cbias[:], start=True, stop=False)
                for q in range(4):
                    mm = pe.matmul(ob_ps, lhs4[:, q], wab[:, q], start=False, stop=(q == 3))
                mm.then_inc(ob_done, 1)

            def turn_x2(t):
                pe.wait_ge(x2_ready, t + 1)
                at_least(pe, h_ready, t)
                for k in range(KD):
                    mm = pe.transpose(tp2_ps[:, k * P:(k + 1) * P], x2[:, k * P:(k + 1) * P], ident[:])
                mm.then_inc(tp2_done, 1)

            def similar(t, gs=range(4)):
                if 0 in gs:
                    wait_apart(pe, x2lo_ready, t + 1, apart_pe)
                for g in gs:
                    if type(t) is int and t == 0:
                        pe.wait_ge(lo_split, g + 1)
                    at_least(pe, sim_ready, 4 * t + g - 1)
                    for k in range(KD):
                        for lhs, rhs in ((x2t_hi, wsim_hi), (x2t_hi, wsim_lo), (x2t_lo, wsim_hi)):
                            first = k == 0 and lhs is x2t_hi and rhs is wsim_hi
                            mm = pe.matmul(sim_ps[g % 2][:].rearrange("p a k -> p (a k)"), lhs[:, k],
                                           rhs[:, k, g * 512:(g + 1) * 512], start=first,
                                           stop=(k == KD - 1 and lhs is x2t_lo))
                    mm.then_inc(sim_done, 1)

            def descend(t):
                pe.wait_ge(x2t_ready, t + 1)
                for k in range(KD):
                    mm = pe.matmul(h_ps, x2t[:, k], down_sb[:, k], start=(k == 0), stop=(k == KD - 1))
                mm.then_inc(h_done, 1)

            def turn_w(t):
                at_least(pe, up_kept, t)
                wait_apart(pe, w_ready, t + 1, apart_pe)
                pe.transpose(wt_ps, w[:], ident[:]).then_inc(wt_done, 1)

            def ascend(t):
                pe.wait_ge(wt_ready, t + 1)
                pe.matmul(up_ps[:, 0:D], wt[:], up_sb[:], start=True, stop=True).then_inc(up_done, 1)

            def step(i, b, live):
                if live(1):
                    similar(i + 1, (0,))
                if live(-2):
                    turn_w(i - 2)
                if live(1):
                    similar(i + 1, (1,))
                if live(2):
                    turn(i + 2, b)
                if live(1):
                    similar(i + 1, (2,))
                if live(2):
                    combine(i + 2)
                if live(-2):
                    ascend(i - 2)
                if live(1):
                    similar(i + 1, (3,))
                    descend(i + 1)
                if live(3):
                    aggregate(i + 3, 1 - b, 0, 14)
                if live(2):
                    turn_x2(i + 2)
                if live(3):
                    aggregate(i + 3, 1 - b, 14, T).then_inc(agg_done, 1)

            pe.wait_ge(ident_ready, 1)
            aggregate(0, 0, 0, T).then_inc(agg_done, 1)
            fold_sim(0)
            fold_sim(1)
            turn(0, 0)
            fold_sim(2)
            fold_sim(3)
            pe.wait_ge(bias_in, 16)
            combine(0)
            for n in range(4, 8):
                fold_sim(n)
            aggregate(1, 1, 0, 9)
            pe.wait_ge(max_step, 9)
            pe.matmul(up_ps[0:1, 0:P], max1[:], ident[:], start=True, stop=True).then_inc(max_turned, 1)
            aggregate(1, 1, 9, 14)
            pe.wait_ge(max_step, 10)
            pe.matmul(up_ps[:, P:P + 1], ones_row, max0[:], start=True, stop=True).then_inc(max_spread, 1)
            turn_x2(0)
            aggregate(1, 1, 14, T).then_inc(agg_done, 1)
            pe.wait_ge(expert_in, 32)
            tiles_loop(pe, -1, T + 1, (-2, 3), step)


def kernel(x, adj, L0_gnn_W_self, L0_gnn_b_self, L0_gnn_W_nb, L0_gnn_b_nb, L0_gnn_W_comb, L0_gnn_b_comb,
           L0_ffn_W_q, L0_ffn_keys, L0_ffn_down_embed, L0_ffn_up_embed):
    import numpy as _np
    import concourse.bacc as _bacc
    from concourse import mybir as _mybir
    from concourse.bass_utils import run_bass_kernel_spmd as _run

    x, adj = _np.asarray(x), _np.asarray(adj)
    n = x.shape[0]
    tiles = -(-n // P)
    square = _np.zeros((tiles * P, tiles * P), adj.dtype)
    square[:n, :n] = adj
    adj_t = square.reshape(tiles, P, tiles, P).transpose(0, 3, 2, 1)
    wq_t = _np.asarray(L0_ffn_W_q).T.reshape(2 * HEADS, P, D).transpose(1, 0, 2)
    keys_t = _np.asarray(L0_ffn_keys).transpose(3, 2, 0, 1).reshape(P, 2 * HEADS, KEYS)
    b_self, b_nb = _np.asarray(L0_gnn_b_self), _np.asarray(L0_gnn_b_nb)
    bcols = _np.concatenate([b_self, b_nb]).reshape(4, P).T
    given = {
        "x": x,
        "adj_t": adj_t,
        "wself_t": _np.asarray(L0_gnn_W_self).T,
        "wnb_t": _np.asarray(L0_gnn_W_nb).T,
        "wcomb": _np.asarray(L0_gnn_W_comb),
        "bcols": bcols,
        "bcomb": _np.asarray(L0_gnn_b_comb).reshape(1, D),
        "wq_t": wq_t,
        "keys_t": keys_t,
        "down_t": _np.asarray(L0_ffn_down_embed)[SLOTS].T,
        "up": _np.asarray(L0_ffn_up_embed)[SLOTS],
    }
    nc = _bacc.Bacc("TRN2", target_bir_lowering=False, num_devices=1)
    arrays, args = {}, []
    for name, a in given.items():
        a = _np.ascontiguousarray(a)
        arrays[f"in_{name}"] = a
        args.append(nc.dram_tensor(f"in_{name}", a.shape, _mybir.dt.from_np(a.dtype), kind="ExternalInput").ap())
    out = nc.dram_tensor("out_x", (n, D), _mybir.dt.float32, kind="ExternalOutput").ap()
    graph_and_experts(nc, *args, out)
    r = _run(nc, [arrays], core_ids=[0])
    return r.results[0]["out_x"]
```
